# Optimizing a Trainium2 kernel written in Bass

```python
import numpy as np
import jax
import jax.numpy as jnp

def _softmax(x, axis=-1):
    return jax.nn.softmax(x, axis=axis)

def _gelu(x):
    return jax.nn.gelu(x, approximate=True)

def _silu(x):
    return jax.nn.silu(x)

def _sigmoid(x):
    return jax.nn.sigmoid(x)

def _layernorm(x, axis=-1, eps=1e-05):
    m = jnp.mean(x, axis=axis, keepdims=True)
    v = jnp.var(x, axis=axis, keepdims=True)
    return (x - m) / jnp.sqrt(v + eps)

def _scatter_add(tgt, idx, src, axis=0):
    return tgt.at[idx].add(src)

def _segment_sum(src, seg, n):
    return jax.ops.segment_sum(src, seg, n)
kernel_name = 'mk_adaln_ffn_d1_seqx_r8_5d811b'

def setup_inputs(seed: int=0):
    np.random.seed(seed)
    _w = jnp.asarray

    def _rec_inputs():
        import jax
        import jax.numpy as jnp
        _rk = jax.random.key(seed)
        x = -7.109e-05 + 0.9999 * jax.random.normal(jax.random.fold_in(_rk, 1), (128, 32, 256), jnp.float32)
        _lenS = 32 - jax.random.randint(jax.random.fold_in(_rk, 7), (128,), 0, max(1, 32 // 4) + 1, jnp.int32)
        _lenS2 = 32 - jax.random.randint(jax.random.fold_in(_rk, 8), (128,), 0, max(1, 32 // 4) + 1, jnp.int32)
        itok_B_1_198 = jax.random.randint(jax.random.fold_in(_rk, 11), (128,), 1, 199, jnp.int32)
        return (x, itok_B_1_198)
    x, itok_B_1_198 = _rec_inputs()

    def _L0_cond_setup():
        import jax, jax.numpy as jnp
        import numpy as np
        B, C, T = (128, 32, 256)
        S, D = (200, 32)
        key = jax.random.key(seed)
        k1, k2, k3 = jax.random.split(key, 3)
        x = jax.random.normal(k1, (B, C, T), dtype=jnp.float32)
        conditions = jax.random.randint(k2, (B,), 0, S, dtype=jnp.int64)
        weights = jax.random.normal(k3, (S, C, D), dtype=jnp.float32) / jnp.sqrt(jnp.float32(C))
        return {'x': x, 'conditions': conditions, 'weights': weights}
    _L0_cond_all = _L0_cond_setup()
    _L0_cond_in = {k: v for k, v in _L0_cond_all.items() if k in ('weights',)}
    del _L0_cond_all

    def _L0_ffn_setup():
        import jax, jax.numpy as jnp
        import numpy as np
        HID = 256
        INTER = 1024
        NEXP = 8
        TOPK = 2
        EPS = 1e-05

        def _mock_fused_moe(x, selected_experts, routing_weights, expert_weight):
            y = jnp.einsum('bsh,hd->bsd', x, expert_weight)
            scale = routing_weights.sum(axis=-1, keepdims=True)
            return y * scale
        key = jax.random.key(seed)
        ks = jax.random.split(key, 6)
        s = lambda fan_in: 1.0 / np.sqrt(fan_in)
        return {'hidden_states': jax.random.normal(ks[0], (4, 512, HID), dtype=jnp.float32), 'gate_w': jax.random.uniform(ks[1], (HID, NEXP), jnp.float32, -s(HID), s(HID)), 'up_w': jax.random.uniform(ks[2], (HID, INTER), jnp.float32, -s(HID), s(HID)), 'down_w': jax.random.uniform(ks[3], (INTER, HID), jnp.float32, -s(INTER), s(INTER)), 'expert_weight': jax.random.normal(ks[4], (HID, HID), dtype=jnp.float32), 'ln_gamma': jnp.ones((HID,), jnp.float32), 'ln_beta': jnp.zeros((HID,), jnp.float32)}
    _L0_ffn_all = _L0_ffn_setup()
    _L0_ffn_in = {k: v for k, v in _L0_ffn_all.items() if k in ('gate_w', 'up_w', 'down_w', 'expert_weight', 'ln_gamma', 'ln_beta')}
    del _L0_ffn_all
    return {'x': x, 'itok_B_1_198': itok_B_1_198, 'L0_cond_weights': _L0_cond_in['weights'], 'L0_ffn_gate_w': _L0_ffn_in['gate_w'], 'L0_ffn_up_w': _L0_ffn_in['up_w'], 'L0_ffn_down_w': _L0_ffn_in['down_w'], 'L0_ffn_expert_weight': _L0_ffn_in['expert_weight'], 'L0_ffn_ln_gamma': _L0_ffn_in['ln_gamma'], 'L0_ffn_ln_beta': _L0_ffn_in['ln_beta']}

def reference(x, itok_B_1_198, L0_cond_weights, L0_ffn_gate_w, L0_ffn_up_w, L0_ffn_down_w, L0_ffn_expert_weight, L0_ffn_ln_gamma, L0_ffn_ln_beta):
    import jax
    import jax.numpy as jnp

    def _L0_cond_ref(x, conditions, weights):
        import jax, jax.numpy as jnp
        import numpy as np
        B, C, T = (128, 32, 256)
        S, D = (200, 32)
        w = weights[conditions]
        return jnp.einsum('bct,bcd->bdt', x, w)

    def _L0_ffn_ref(hidden_states, gate_w, up_w, down_w, expert_weight, ln_gamma, ln_beta):
        import jax, jax.numpy as jnp
        import numpy as np
        HID = 256
        INTER = 1024
        NEXP = 8
        TOPK = 2
        EPS = 1e-05

        def _mock_fused_moe(x, selected_experts, routing_weights, expert_weight):
            y = jnp.einsum('bsh,hd->bsd', x, expert_weight)
            scale = routing_weights.sum(axis=-1, keepdims=True)
            return y * scale
        residuals = hidden_states
        logits = jnp.einsum('bsh,he->bse', hidden_states, gate_w)
        routing_weights, selected_experts = jax.lax.top_k(logits, TOPK)
        h = jnp.einsum('bsh,hi->bsi', residuals, up_w)
        h = jnp.square(jax.nn.relu(h))
        shared_out = jnp.einsum('bsi,ih->bsh', h, down_w)
        moe_out = _mock_fused_moe(hidden_states, selected_experts, routing_weights, expert_weight)
        y = shared_out + moe_out
        mu = y.mean(axis=-1, keepdims=True)
        var = jnp.mean(jnp.square(y - mu), axis=-1, keepdims=True)
        return (y - mu) * jax.lax.rsqrt(var + EPS) * ln_gamma + ln_beta
    x = x + _L0_ffn_ref(_L0_cond_ref(x, itok_B_1_198, L0_cond_weights), L0_ffn_gate_w, L0_ffn_up_w, L0_ffn_down_w, L0_ffn_expert_weight, L0_ffn_ln_gamma, L0_ffn_ln_beta)
    return x

_drawn_inputs = setup_inputs


def setup_inputs(seed=0):
    import zlib

    import numpy as np

    out = dict(_drawn_inputs(seed))
    spreads = {'L0_ffn_ln_gamma': (1.0, 0.2), 'L0_ffn_ln_beta': (0.0, 0.1)}
    factors = {}
    for name, (base, spread) in spreads.items():
        noise = np.random.default_rng([zlib.crc32(name.encode()), seed]).standard_normal(out[name].shape)
        drawn = base * np.exp(spread * noise) if base else spread * noise
        out[name] = jnp.asarray(drawn.astype(out[name].dtype))
    for name, factor in factors.items():
        out[name] = (out[name] * factor).astype(out[name].dtype)
    return out
```

```python
from contextlib import ExitStack

import concourse.bass as bass
from concourse import mybir

P = 128
ROWS_B, C, T, D = 128, 32, 256, 32
INTER, NEXP = 1024, 8
EPS = 1e-5
Q = P // C
GROUPS = ROWS_B // Q
TILES = 4
BLOCKS = GROUPS // TILES
TOK = TILES * P
K = T // P
CH = INTER // P
EG = T + NEXP
UPB = 4
HALF = CH // 2


def adaln_ffn(nc, x, cond, cond_w, gate_w, up_w, down_w, expert_w, gamma, beta, out):
    f32, f32r, i32 = mybir.dt.float32, mybir.dt.float32r, mybir.dt.int32
    ALU, ACT = mybir.AluOpType, mybir.ActivationFunctionType

    x_rows = x.rearrange("b c t -> (b c) t").rearrange("(g p) t -> p g t", p=P)
    out_rows = out.rearrange("b c t -> (b c) t").rearrange("(g p) t -> p g t", p=P)
    table = cond_w.rearrange("s c d -> (s c) d")

    ctx = ExitStack()
    with ctx:
        def sb(name, shape, dt=f32):
            return ctx.enter_context(nc.sbuf_tensor(name, shape, dt))

        def bank(name):
            return ctx.enter_context(nc.psum_tensor(name, [P, 512], f32))

        def sem(name):
            return ctx.enter_context(nc.semaphore(name))

        up_hi = sb("up_hi", [P, K, INTER], f32r)
        up_lo = sb("up_lo", [P, K, INTER], f32r)
        down_hl = sb("down_hl", [P, CH, 2, T], f32r)
        eg_hi = sb("eg_hi", [P, K, EG], f32r)
        eg_lo = sb("eg_lo", [P, K, EG], f32r)
        down_raw = sb("down_raw", [P, CH, T])
        eg_raw = sb("eg_raw", [P, K, EG])
        gamma_b = sb("gamma_b", [P, T])
        beta_b = sb("beta_b", [P, T])
        x_sb = sb("x_sb", [P, GROUPS, T])
        cond_b = sb("cond_b", [P, ROWS_B], i32)
        chan = sb("chan", [P, Q], i32)
        rows = sb("rows", [P, GROUPS], i32)
        w_raw = sb("w_raw", [P, GROUPS, D])
        w_hi = sb("w_hi", [P, GROUPS, D])
        mask = sb("mask", [P, TILES, Q, D])
        wd_hi = sb("wd_hi", [P, TILES, Q, D], f32r)
        wd_lo = sb("wd_lo", [P, TILES, Q, D], f32r)
        xs_hi = sb("xs_hi", [P, TILES, T], f32r)
        xs_lo = sb("xs_lo", [P, TILES, T], f32r)
        hid_hi = sb("hid_hi", [P, 2, K, TOK], f32r)
        hid_lo = sb("hid_lo", [P, 2, K, TOK], f32r)
        relu = sb("relu", [P, 2, TOK])
        square = sb("square", [P, 2, TOK])
        sq_hi = sb("sq_hi", [P, 2, CH, TOK], f32r)
        sq_lo = sb("sq_lo", [P, 2, CH, TOK], f32r)
        top8 = sb("top8", [P, 8])
        scale = sb("scale", [P, 2])
        moe = sb("moe", [P, TILES, T])
        y_half = sb("y_half", [P, T])
        y = sb("y", [P, 2, T])
        stats = sb("stats", [P, 6])
        meanvar = sb("meanvar", [P, 2, 2])
        var_eps = sb("var_eps", [P, 2])
        minus_half = sb("minus_half", [P, 1])
        eps = sb("eps", [P, 1])
        rstd = sb("rstd", [P, 2])
        result = sb("result", [P, 2, TILES, T])
        up_raw = result[:, :, :, :].rearrange("p a b t -> p (a b t)").rearrange("p (k i) -> p k i", k=K)

        up_ps = [bank(f"up_ps{n}") for n in range(UPB)]
        hid_ps = bank("hid_ps")
        moe_ps = bank("moe_ps")
        down_ps = [bank(f"down_ps{n}") for n in range(2)]

        x_landed = [sem("x_landed_even"), sem("x_landed_odd")]
        cond_landed, down_landed, eg_landed, ln_landed = map(
            sem, ("cond_landed", "down_landed", "eg_landed", "ln_landed"))
        gathered_first, gathered_rest = sem("gathered_first"), sem("gathered_rest")
        result_moved = [sem("result_moved_even"), sem("result_moved_odd")]
        chan_ready, rows_ready, zeroed, mask_ready, consts_ready = map(
            sem, ("chan_ready", "rows_ready", "zeroed", "mask_ready", "consts_ready"))
        up_hi_ready, up_lo_ready, down_hi_ready, down_lo_ready, eg_hi_ready, eg_lo_ready = map(
            sem, ("up_hi_ready", "up_lo_ready", "down_hi_ready", "down_lo_ready", "eg_hi_ready", "eg_lo_ready"))
        w_hi_ready, w_lo_ready = sem("w_hi_ready"), sem("w_lo_ready")
        up_done, down_done, moe_done, hid_done = map(sem, ("up_done", "down_done", "moe_done", "hid_done"))
        relu_done, sq_hi_done, hid_hi_done, moe_scaled, x_hi_done = map(
            sem, ("relu_done", "sq_hi_done", "hid_hi_done", "moe_scaled", "x_hi_done"))
        square_done, hid_lo_done, top8_done, scale_done, wd_done = map(
            sem, ("square_done", "hid_lo_done", "top8_done", "scale_done", "wd_done"))
        y_half_done, y_done, bn_done, stats_done, scaled_done, result_done = map(
            sem, ("y_half_done", "y_done", "bn_done", "stats_done", "scaled_done", "result_done"))
        sq_lo_done, x_lo_done, xb_done, var_eps_done, rstd_done = map(
            sem, ("sq_lo_done", "x_lo_done", "xb_done", "var_eps_done", "rstd_done"))

        def wait(eng, s, count):
            if not isinstance(count, int) or count > 0:
                eng.wait_ge(s, count)

        def wait_apart(eng, s, count, settled, settled_at):
            eng.wait_ge(settled, settled_at)
            eng.wait_ge(s, count)

        def steps(eng, step):
            step(0, 0)
            with eng.Fori(0, BLOCKS // 2 - 1) as i:
                step(2 * i + 1, 1)
                step(2 * i + 2, 0)
            step(BLOCKS - 1, 1)
            step(BLOCKS, 0)

        def first(j):
            return isinstance(j, int) and j == 0

        def has_up(j):
            return not isinstance(j, int) or j < BLOCKS

        def has_next(j):
            return not isinstance(j, int) or j + 1 < BLOCKS

        def groups(j):
            return slice(TILES * j, TILES * j + TILES) if isinstance(j, int) else bass.ds(TILES * j, TILES)

        def group(j, t):
            return slice(TILES * j + t, TILES * j + t + 1) if isinstance(j, int) else bass.ds(TILES * j + t, 1)

        block = ctx.enter_context(nc.Block())

        @block.sync
        def _(sp):
            sp.dma_start(cond_b[:, :], cond.rearrange("(o b) -> o b", o=1).to_broadcast([P, ROWS_B])) \
                .then_inc(cond_landed, 16)
            for j in range(2):
                sp.dma_start(x_sb[:, groups(j), :], x_rows[:, groups(j), :]).then_inc(x_landed[j], 16)
            sp.dma_start(down_raw[:, :, :], down_w.rearrange("(c p) h -> p c h", p=P)).then_inc(down_landed, 16)
            sp.dma_start(gamma_b[:, :], gamma.rearrange("(o t) -> o t", o=1).to_broadcast([P, T])) \
                .then_inc(ln_landed, 16)
            sp.dma_start(beta_b[:, :], beta.rearrange("(o t) -> o t", o=1).to_broadcast([P, T])) \
                .then_inc(ln_landed, 16)
            with sp.Fori(1, BLOCKS // 2) as i:
                for par in range(2):
                    sp.wait_ge(x_landed[par], 16 * i)
                    sp.dma_start(x_sb[:, groups(2 * i + par), :], x_rows[:, groups(2 * i + par), :]) \
                        .then_inc(x_landed[par], 16)

            def store(j, par):
                sp.wait_ge(result_done, TILES * j + TILES)
                sp.dma_start(out_rows[:, groups(j), :], result[:, par, :, :]).then_inc(result_moved[par], 16)

            with sp.Fori(0, BLOCKS // 2 - 1) as i:
                store(2 * i, 0)
                store(2 * i + 1, 1)
            store(BLOCKS - 2, 0)
            for t in range(TILES):
                j = BLOCKS - 1
                sp.wait_ge(result_done, TILES * j + t + 1)
                sp.dma_start(out_rows[:, group(j, t), :], result[:, 1, t:t + 1, :]).then_inc(result_moved[1], 16)
            sp.wait_ge(result_moved[0], 16 * (BLOCKS // 2 + 1))
            sp.wait_ge(result_moved[1], 16 * (BLOCKS // 2 + TILES))

        @block.tensor
        def _(pe):
            def conditioning(j, par, k):
                if k == 0:
                    pe.wait_ge(x_hi_done, j + 1)
                    pe.wait_ge(x_lo_done, j + 1)
                    pe.wait_ge(wd_done, 2 * j + 2)
                wait(pe, hid_hi_done, K * j + k)
                wait(pe, hid_lo_done, K * j + k)
                for t in range(TILES):
                    dst = hid_ps[:, P * t:P * t + P]
                    a_hi = xs_hi[:, t, P * k:P * k + P]
                    a_lo = xs_lo[:, t, P * k:P * k + P]
                    b_hi = wd_hi[:, t, :, :].rearrange("p q d -> p (q d)")
                    b_lo = wd_lo[:, t, :, :].rearrange("p q d -> p (q d)")
                    pe.matmul(dst, a_lo, b_hi, start=True, stop=False)
                    pe.matmul(dst, a_hi, b_lo, start=False, stop=False)
                    mm = pe.matmul(dst, a_hi, b_hi, start=False, stop=True)
                mm.then_inc(hid_done, 1)

            def up(j, par, c):
                if c == 0:
                    pe.wait_ge(hid_hi_done, K * j + K)
                    pe.wait_ge(hid_lo_done, K * j + K)
                if first(j) and c in (0, HALF):
                    pe.wait_ge(up_hi_ready, 1 + c // HALF)
                    pe.wait_ge(up_lo_ready, 1 + c // HALF)
                wait(pe, square_done, CH * j + c - UPB + 1)
                dst = up_ps[c % UPB][:, :]
                for k in range(K):
                    w_h = up_hi[:, k, P * c:P * c + P]
                    w_l = up_lo[:, k, P * c:P * c + P]
                    pe.matmul(dst, w_l, hid_hi[:, par, k, :], start=(k == 0), stop=False)
                    pe.matmul(dst, w_h, hid_lo[:, par, k, :], start=False, stop=False)
                    mm = pe.matmul(dst, w_h, hid_hi[:, par, k, :], start=False, stop=(k == K - 1))
                mm.then_inc(up_done, 1)

            def down(j, par, t, half):
                if half == 0:
                    if first(j) and t == 0:
                        pe.wait_ge(down_hi_ready, 1)
                        pe.wait_ge(down_lo_ready, 1)
                    if t > 0:
                        wait(pe, y_done, TILES * j + t - 1)
                if t == 0:
                    pe.wait_ge(sq_hi_done, CH * j + HALF * (half + 1))
                    pe.wait_ge(sq_lo_done, CH * j + HALF * (half + 1))
                dst = down_ps[t % 2]
                for c in range(HALF * half, HALF * half + HALF):
                    pe.matmul(dst[:, :], sq_hi[:, par, c, P * t:P * t + P],
                              down_hl[:, c, :, :].rearrange("p s t -> p (s t)"),
                              start=(c == 0), stop=False)
                    mm = pe.matmul(dst[:, T:2 * T], sq_lo[:, par, c, P * t:P * t + P], down_hl[:, c, 0, :],
                                   start=False, stop=(c == CH - 1))
                if half == 1:
                    mm.then_inc(down_done, 1)

            def experts(j, par, t):
                if first(j) and t == 0:
                    pe.wait_ge(eg_hi_ready, 1)
                    pe.wait_ge(eg_lo_ready, 1)
                wait(pe, moe_scaled, TILES * j + t)
                dst = moe_ps[:, 0:EG]
                for k in range(K):
                    a_hi = hid_hi[:, par, k, P * t:P * t + P]
                    a_lo = hid_lo[:, par, k, P * t:P * t + P]
                    pe.matmul(dst, a_lo, eg_hi[:, k, :], start=(k == 0), stop=False)
                    pe.matmul(dst, a_hi, eg_lo[:, k, :], start=False, stop=False)
                    mm = pe.matmul(dst, a_hi, eg_hi[:, k, :], start=False, stop=(k == K - 1))
                mm.then_inc(moe_done, 1)

            def step(j, par):
                for c in range(CH):
                    if has_up(j):
                        up(j, par, c)
                    if not first(j):
                        down(j - 1, 1 - par, c // 2, c % 2)
                    if has_up(j) and c % 2 == 1:
                        experts(j, par, c // 2)
                    if has_next(j) and c in (2, 5):
                        conditioning(j + 1, 1 - par, c // 4)

            conditioning(0, 0, 0)
            conditioning(0, 0, 1)
            steps(pe, step)

        @block.scalar
        def _(act):
            for k in range(K):
                act.dma_start(up_raw[:, k, :], up_w[P * k:P * k + P, :]).then_inc(result_moved[k], 16)
            act.dma_start(eg_raw[:, :, 0:T], expert_w.rearrange("(k p) h -> p k h", p=P)).then_inc(eg_landed, 16)
            act.dma_start(eg_raw[:, :, T:EG], gate_w.rearrange("(k p) e -> p k e", p=P)).then_inc(eg_landed, 16)

            def split_x(j, par):
                act.wait_ge(x_landed[par], 16 * (j // 2 + 1) if isinstance(j, int) else 8 * (j - par) + 16)
                wait(act, hid_done, K * j)
                act.activation(xs_hi[:, :, :], x_sb[:, groups(j), :], ACT.Copy).then_inc(x_hi_done, 1)

            def hidden(j, par, k):
                act.wait_ge(hid_done, K * j + k + 1)
                act.activation(hid_hi[:, par, k, :], hid_ps[:, :], ACT.Copy).then_inc(hid_hi_done, 1)

            def scale_moe(j, t):
                act.wait_ge(scale_done, TILES * j + t + 1)
                wait(act, y_done, TILES * (j - 1) + t + 1)
                act.activation(moe[:, t, :], moe_ps[:, 0:T], ACT.Copy, scale=scale[:, t % 2:t % 2 + 1]) \
                    .then_inc(moe_scaled, 1)

            def step(j, par):
                for c in range(CH):
                    if has_next(j) and c == 0:
                        split_x(j + 1, 1 - par)
                    if has_next(j) and c in (3, 6):
                        hidden(j + 1, 1 - par, c // 6)
                    if has_up(j):
                        n = CH * j + c
                        act.wait_ge(up_done, n + 1)
                        wait(act, square_done, n - 1)
                        act.activation(relu[:, c % 2, :], up_ps[c % UPB][:, :], ACT.Relu).then_inc(relu_done, 1)
                    if has_up(j) and c % 2 == 0 and c > 0:
                        scale_moe(j, c // 2 - 1)
                    if not first(j) and c == 0:
                        scale_moe(j - 1, TILES - 1)
                    if has_up(j):
                        act.wait_ge(relu_done, n + 1)
                        act.activation(sq_hi[:, par, c, :], relu[:, c % 2, :], ACT.Square) \
                            .then_inc(sq_hi_done, 1)

            split_x(0, 0)
            act.wait_ge(gathered_first, 16 * TILES)
            act.activation(w_hi[:, 0:TILES, :].bitcast(f32r), w_raw[:, 0:TILES, :], ACT.Copy) \
                .then_inc(w_hi_ready, 1)
            for k in range(K):
                act.wait_ge(result_moved[k], 16)
            for h in range(2):
                cols = slice(h * INTER // 2, (h + 1) * INTER // 2)
                act.activation(up_hi[:, :, cols], up_raw[:, :, cols], ACT.Copy).then_inc(up_hi_ready, 1)
            hidden(0, 0, 0)
            hidden(0, 0, 1)
            act.wait_ge(gathered_rest, 16 * (GROUPS - TILES))
            act.activation(w_hi[:, TILES:GROUPS, :].bitcast(f32r), w_raw[:, TILES:GROUPS, :], ACT.Copy) \
                .then_inc(w_hi_ready, 1)
            act.wait_ge(eg_landed, 32)
            act.activation(eg_hi[:, :, :], eg_raw[:, :, :], ACT.Copy).then_inc(eg_hi_ready, 1)
            act.wait_ge(down_landed, 16)
            act.activation(down_hl[:, :, 0, :], down_raw[:, :, :], ACT.Copy).then_inc(down_hi_ready, 1)
            steps(act, step)

        @block.vector
        def _(dve):
            def gather_rows():
                dve.wait_ge(cond_landed, 16)
                dve.wait_ge(chan_ready, 1)
                of_batch = cond_b[:, :].rearrange("p (g q) -> p g q", q=Q)
                for q in range(Q):
                    part = slice(C * q, C * q + C)
                    dve.tensor_scalar(rows[part, :], of_batch[part, :, q], float(C), chan[part, q:q + 1],
                                      ALU.mult, ALU.add).then_inc(rows_ready, 1)

            def split_w(n, g0, g1):
                dve.wait_ge(w_hi_ready, n)
                dve.tensor_tensor(w_raw[:, g0:g1, :], w_raw[:, g0:g1, :], w_hi[:, g0:g1, :], ALU.subtract) \
                    .then_inc(w_lo_ready, 1)

            def spread_w(j):
                if not isinstance(j, int) or j > 0:
                    dve.wait_ge(w_lo_ready, 2)
                else:
                    dve.wait_ge(w_lo_ready, 1)
                wait(dve, hid_done, K * j)
                for dst, src in ((wd_hi, w_hi), (wd_lo, w_raw)):
                    wide = src[:, groups(j), :].unsqueeze(2).to_broadcast([P, TILES, Q, D])
                    dve.tensor_tensor(dst[:, :, :, :], wide, mask[:, :, :, :], ALU.mult).then_inc(wd_done, 1)

            def hidden(j, par, k):
                dve.wait_ge(hid_hi_done, K * j + k + 1)
                dve.tensor_tensor(hid_lo[:, par, k, :], hid_ps[:, :], hid_hi[:, par, k, :].bitcast(f32),
                                  ALU.subtract).then_inc(hid_lo_done, 1)

            def gate(j, t):
                n = TILES * j + t
                if isinstance(j, int) and j == BLOCKS - 1 and t == TILES - 1:
                    dve.wait_ge(moe_done, n + 1)
                dve.max(top8[:, :], moe_ps[:, T:EG]).then_inc(top8_done, 1)
                dve.wait_ge(top8_done, n + 1)
                wait(dve, moe_scaled, n - 1)
                dve.tensor_tensor(scale[:, t % 2:t % 2 + 1], top8[:, 0:1], top8[:, 1:2], ALU.add) \
                    .then_inc(scale_done, 1)

            def total(j, t):
                n = TILES * j + t
                dve.wait_ge(down_done, n + 1)
                dve.wait_ge(moe_scaled, n + 1)
                dve.tensor_tensor(y_half[:, :], down_ps[t % 2][:, T:2 * T], moe[:, t, :], ALU.add) \
                    .then_inc(y_half_done, 1)
                dve.wait_ge(y_half_done, n + 1)
                dve.tensor_tensor(y[:, t % 2, :], down_ps[t % 2][:, 0:T], y_half[:, :], ALU.add) \
                    .then_inc(y_done, 1)
                dve.wait_ge(y_done, n + 1)
                dve.bn_stats(stats[:, :], y[:, t % 2, :]).then_inc(bn_done, 1)
                wait_apart(dve, bn_done, n + 1, mask_ready, Q)
                dve.bn_aggr(meanvar[:, t % 2, :], stats[:, :]).then_inc(stats_done, 1)

            def finish(j, par, t):
                n = TILES * j + t
                dve.wait_ge(stats_done, n + 1)
                dve.scalar_tensor_tensor(y[:, t % 2, :], y[:, t % 2, :], meanvar[:, t % 2, 0:1], gamma_b[:, :],
                                         ALU.subtract, ALU.mult).then_inc(scaled_done, 1)
                dve.wait_ge(scaled_done, n + 1)
                dve.wait_ge(rstd_done, n + 1)
                dve.wait_ge(xb_done, j + 1)
                if t == 0:
                    dve.wait_ge(result_moved[par], 16 * (j // 2) + 16 if isinstance(j, int) else 8 * (j - par) + 16)
                dve.scalar_tensor_tensor(result[:, par, t, :], y[:, t % 2, :], rstd[:, t % 2:t % 2 + 1],
                                         x_sb[:, group(j, t), :].rearrange("p o t -> p (o t)"),
                                         ALU.mult, ALU.add).then_inc(result_done, 1)

            def step(j, par):
                for c in range(CH):
                    if has_next(j) and c in (3, 6):
                        hidden(j + 1, 1 - par, c // 6)
                    if has_up(j):
                        n = CH * j + c
                        dve.wait_ge(relu_done, n + 1)
                        wait(dve, sq_lo_done, n - 1)
                        dve.scalar_tensor_tensor(square[:, c % 2, :], up_ps[c % UPB][:, :], 0.0,
                                                 relu[:, c % 2, :], ALU.max, ALU.mult).then_inc(square_done, 1)
                    if has_up(j) and c % 2 == 0 and c > 0:
                        gate(j, c // 2 - 1)
                    if not first(j) and c == 0:
                        gate(j - 1, TILES - 1)
                    if has_next(j) and c == 0:
                        spread_w(j + 1)
                    if not first(j) and c % 2 == 1:
                        total(j - 1, c // 2)
                        if c > 1:
                            finish(j - 1, 1 - par, c // 2 - 1)
                if not first(j):
                    finish(j - 1, 1 - par, TILES - 1)

            gather_rows()
            dve.memset(mask[:, :, :, :], 0.0).then_inc(zeroed, 1)
            dve.wait_ge(zeroed, 1)
            for q in range(Q):
                dve.memset(mask[C * q:C * q + C, :, q, :], 1.0).then_inc(mask_ready, 1)
            dve.wait_ge(mask_ready, Q)
            split_w(1, 0, TILES)
            spread_w(0)
            for h in range(2):
                cols = slice(h * INTER // 2, (h + 1) * INTER // 2)
                dve.wait_ge(up_hi_ready, h + 1)
                dve.tensor_tensor(up_lo[:, :, cols], up_raw[:, :, cols], up_hi[:, :, cols].bitcast(f32),
                                  ALU.subtract).then_inc(up_lo_ready, 1)
            hidden(0, 0, 0)
            hidden(0, 0, 1)
            split_w(2, TILES, GROUPS)
            dve.wait_ge(eg_hi_ready, 1)
            dve.tensor_tensor(eg_lo[:, :, :], eg_raw[:, :, :], eg_hi[:, :, :].bitcast(f32), ALU.subtract) \
                .then_inc(eg_lo_ready, 1)
            dve.wait_ge(down_hi_ready, 1)
            dve.tensor_tensor(down_hl[:, :, 1, :], down_raw[:, :, :], down_hl[:, :, 0, :].bitcast(f32),
                              ALU.subtract).then_inc(down_lo_ready, 1)
            dve.wait_ge(ln_landed, 32)
            steps(dve, step)

        @block.gpsimd
        def _(pool):
            def gather(g, landed):
                pool.indirect_dma_start(
                    out=w_raw[:, g, :], out_offset=None, in_=table,
                    in_offset=bass.IndirectOffsetOnAxis(ap=rows[:, g:g + 1], axis=0)).then_inc(landed, 16)

            def split_x(j):
                wait_apart(pool, x_hi_done, j + 1, consts_ready, 2)
                pool.tensor_tensor(xs_lo[:, :, :], x_sb[:, groups(j), :], xs_hi[:, :, :].bitcast(f32),
                                   ALU.subtract).then_inc(x_lo_done, 1)

            def add_beta(j):
                wait_apart(pool, x_lo_done, j + 1, ln_landed, 32)
                pool.tensor_tensor(x_sb[:, groups(j), :], x_sb[:, groups(j), :],
                                   beta_b[:, :].unsqueeze(1).to_broadcast([P, TILES, T]),
                                   ALU.add).then_inc(xb_done, 1)

            def inverse_std(j, t):
                n = TILES * j + t
                pool.wait_ge(stats_done, n + 1)
                pool.tensor_tensor(var_eps[:, t % 2:t % 2 + 1], meanvar[:, t % 2, 1:2], eps[:, :], ALU.add) \
                    .then_inc(var_eps_done, 1)
                pool.wait_ge(var_eps_done, n + 1)
                pool.tensor_tensor(rstd[:, t % 2:t % 2 + 1], var_eps[:, t % 2:t % 2 + 1], minus_half[:, :], ALU.pow) \
                    .then_inc(rstd_done, 1)

            def step(j, par):
                for c in range(CH):
                    if has_next(j) and c == 0:
                        split_x(j + 1)
                    if has_up(j):
                        n = CH * j + c
                        pool.wait_ge(square_done, n + 1)
                        pool.wait_ge(sq_hi_done, n + 1)
                        pool.tensor_tensor(sq_lo[:, par, c, :], square[:, c % 2, :],
                                           sq_hi[:, par, c, :].bitcast(f32), ALU.subtract).then_inc(sq_lo_done, 1)
                    if not first(j) and c % 2 == 0 and c > 0:
                        inverse_std(j - 1, c // 2 - 1)
                    if has_up(j) and c == 3:
                        add_beta(j)
                if not first(j):
                    inverse_std(j - 1, TILES - 1)

            pool.iota(chan[:, :], pattern=[[-C, Q]], base=0, channel_multiplier=1).then_inc(chan_ready, 1)
            pool.memset(minus_half[:, :], -0.5).then_inc(consts_ready, 1)
            pool.memset(eps[:, :], EPS).then_inc(consts_ready, 1)
            pool.wait_ge(rows_ready, Q)
            for g in range(TILES):
                gather(g, gathered_first)
            split_x(0)
            for g in range(TILES, GROUPS):
                gather(g, gathered_rest)
            pool.wait_ge(ln_landed, 32)
            pool.wait_ge(consts_ready, 2)
            steps(pool, step)


_INS = ["x", "itok_B_1_198", "L0_cond_weights", "L0_ffn_gate_w", "L0_ffn_up_w", "L0_ffn_down_w",
        "L0_ffn_expert_weight", "L0_ffn_ln_gamma", "L0_ffn_ln_beta"]
_OUT = ((ROWS_B, C, T), "float32")


def kernel(**inputs):
    import numpy as _np
    import concourse.bacc as _bacc
    from concourse import mybir as _mybir
    from concourse.bass_utils import run_bass_kernel_spmd as _run

    nc = _bacc.Bacc("TRN2", target_bir_lowering=False, num_devices=1)
    arrays, args = {}, []
    for name in _INS:
        a = _np.ascontiguousarray(inputs[name])
        arrays[f"in_{name}_dram"] = a
        args.append(nc.dram_tensor(f"in_{name}_dram", a.shape, _mybir.dt.from_np(a.dtype), kind="ExternalInput").ap())
    shape, dtype = _OUT
    args.append(nc.dram_tensor("out_0_dram", shape, _mybir.dt.from_np(_np.dtype(dtype)), kind="ExternalOutput").ap())
    adaln_ffn(nc, *args)
    r = _run(nc, [arrays], core_ids=[0])
    return r.results[0]["out_0_dram"]
```

```python
from contextlib import ExitStack

import concourse.bass as bass
from concourse import mybir

P = 128
ROWS_B, C, T, D = 128, 32, 256, 32
INTER, NEXP = 1024, 8
EPS = 1e-5
Q = P // C
GROUPS = ROWS_B // Q
TILES = 4
BLOCKS = GROUPS // TILES
TOK = TILES * P
K = T // P
CH = INTER // P
EG = T + NEXP
UPB = 4
HALF = CH // 2
WARM = 3


def adaln_ffn(nc, x, cond, cond_w, gate_w, up_w, down_w, expert_w, gamma, beta, out):
    f32, f32r, i32 = mybir.dt.float32, mybir.dt.float32r, mybir.dt.int32
    ALU, ACT = mybir.AluOpType, mybir.ActivationFunctionType

    x_rows = x.rearrange("b c t -> (b c) t").rearrange("(g p) t -> p g t", p=P)
    out_rows = out.rearrange("b c t -> (b c) t").rearrange("(g p) t -> p g t", p=P)
    table = cond_w.rearrange("s c d -> (s c) d")

    ctx = ExitStack()
    with ctx:
        def sb(name, shape, dt=f32):
            return ctx.enter_context(nc.sbuf_tensor(name, shape, dt))

        def bank(name):
            return ctx.enter_context(nc.psum_tensor(name, [P, 512], f32))

        def sem(name):
            return ctx.enter_context(nc.semaphore(name))

        up_hi = sb("up_hi", [P, K, INTER], f32r)
        up_lo = sb("up_lo", [P, K, INTER], f32r)
        down_hl = sb("down_hl", [P, CH, 2, T], f32r)
        eg_hi = sb("eg_hi", [P, K, EG], f32r)
        eg_lo = sb("eg_lo", [P, K, EG], f32r)
        down_raw = sb("down_raw", [P, CH, T])
        eg_raw = sb("eg_raw", [P, K, EG])
        gamma_b = sb("gamma_b", [P, T])
        beta_b = sb("beta_b", [P, T])
        x_sb = sb("x_sb", [P, GROUPS, T])
        cond_b = sb("cond_b", [P, TOK // C], i32)
        cond_col = sb("cond_col", [P, 1], i32)
        chan = sb("chan", [P, Q], i32)
        rows = sb("rows", [P, TILES], i32)
        w_raw = sb("w_raw", [P, GROUPS, D])
        w_hi = sb("w_hi", [P, GROUPS, D])
        mask = sb("mask", [P, TILES, Q, D])
        wd_hl = sb("wd_hl", [P, TILES, 2, Q, D], f32r)
        xs_hi = sb("xs_hi", [P, TILES, T], f32r)
        xs_lo = sb("xs_lo", [P, TILES, T], f32r)
        hid_hi = sb("hid_hi", [P, 2, K, TOK], f32r)
        hid_lo = sb("hid_lo", [P, 2, K, TOK], f32r)
        hid_rest = sb("hid_rest", [P, 2, 2, P])
        relu = sb("relu", [P, 2, TOK])
        square = sb("square", [P, 2, TOK])
        sq_hi = sb("sq_hi", [P, 2, CH, TOK], f32r)
        sq_lo = sb("sq_lo", [P, 2, CH, TOK], f32r)
        top8 = sb("top8", [P, 8])
        scale = sb("scale", [P, 2])
        moe = sb("moe", [P, TILES, T])
        y_half = sb("y_half", [P, T])
        y = sb("y", [P, 2, T])
        stats = sb("stats", [P, 6])
        meanvar = sb("meanvar", [P, 2, 2])
        var_eps = sb("var_eps", [P, 2])
        minus_half = sb("minus_half", [P, 1])
        eps = sb("eps", [P, 1])
        rstd = sb("rstd", [P, 2])
        result = sb("result", [P, 2, TILES, T])
        up_raw = result[:, :, :, :].rearrange("p a b t -> p (a b t)").rearrange("p (k i) -> p k i", k=K)

        w_all = moe[:, :, :].rearrange("p a t -> p (a t)")
        w_by_batch = nc.dram_tensor("w_by_batch", [ROWS_B, C * D], f32, kind="Internal").ap()

        up_ps = [bank(f"up_ps{n}") for n in range(UPB)]
        hid_ps = bank("hid_ps")
        moe_ps = bank("moe_ps")
        down_ps = [bank(f"down_ps{n}") for n in range(2)]

        x_landed = [sem("x_landed_even"), sem("x_landed_odd")]
        cond_landed, cond_col_landed, down_landed, eg_landed, ln_landed = map(
            sem, ("cond_landed", "cond_col_landed", "down_landed", "eg_landed", "ln_landed"))
        gathered_first, gathered_all, w_written, w_landed = map(
            sem, ("gathered_first", "gathered_all", "w_written", "w_landed"))
        result_moved = [sem("result_moved_even"), sem("result_moved_odd")]
        chan_ready, rows_ready, zeroed, mask_ready, consts_ready = map(
            sem, ("chan_ready", "rows_ready", "zeroed", "mask_ready", "consts_ready"))
        up_lo_ready = [sem("up_lo_ready_even"), sem("up_lo_ready_odd")]
        up_hi_ready, down_hi_ready, down_lo_ready, eg_hi_ready, eg_lo_ready = map(
            sem, ("up_hi_ready", "down_hi_ready", "down_lo_ready", "eg_hi_ready", "eg_lo_ready"))
        w_hi_ready, w_lo_ready, w_lo_rest_ready = sem("w_hi_ready"), sem("w_lo_ready"), sem("w_lo_rest_ready")
        up_done, down_done, moe_done, hid_done = map(sem, ("up_done", "down_done", "moe_done", "hid_done"))
        relu_done, sq_hi_done, hid_hi_done, moe_scaled, x_hi_done = map(
            sem, ("relu_done", "sq_hi_done", "hid_hi_done", "moe_scaled", "x_hi_done"))
        square_done, hid_rest_done, hid_lo_done, top8_done, scale_done, wd_done = map(
            sem, ("square_done", "hid_rest_done", "hid_lo_done", "top8_done", "scale_done", "wd_done"))
        y_half_done, y_done, bn_done, stats_done, scaled_done, result_done = map(
            sem, ("y_half_done", "y_done", "bn_done", "stats_done", "scaled_done", "result_done"))
        sq_lo_done, x_lo_done, xb_done, var_eps_done, rstd_done = map(
            sem, ("sq_lo_done", "x_lo_done", "xb_done", "var_eps_done", "rstd_done"))

        def wait(eng, s, count):
            if not isinstance(count, int) or count > 0:
                eng.wait_ge(s, count)

        def wait_apart(eng, s, count, settled, settled_at):
            eng.wait_ge(settled, settled_at)
            eng.wait_ge(s, count)

        def steps(eng, step):
            step(0, 0)
            with eng.Fori(0, BLOCKS // 2 - 1) as i:
                step(2 * i + 1, 1)
                step(2 * i + 2, 0)
            step(BLOCKS - 1, 1)
            step(BLOCKS, 0)

        def first(j):
            return isinstance(j, int) and j == 0

        def has_up(j):
            return not isinstance(j, int) or j < BLOCKS

        def has_next(j):
            return not isinstance(j, int) or j + 1 < BLOCKS

        def groups(j):
            return slice(TILES * j, TILES * j + TILES) if isinstance(j, int) else bass.ds(TILES * j, TILES)

        def group(j, t):
            return slice(TILES * j + t, TILES * j + t + 1) if isinstance(j, int) else bass.ds(TILES * j + t, 1)

        def rounds(bank_):
            return bank_[:, :].rearrange("p (g s n) -> p g s n", g=2, s=2)

        ROUNDS = 2 * K
        ROUND_AT = (2, 3, 5, 6)
        first_rounds = {0: [hid_ps, moe_ps, *down_ps], 1: [hid_ps, down_ps[1], hid_ps, down_ps[0]]}
        first_experts = [moe_ps, *down_ps, moe_ps]

        def round_bank(j, r):
            return rounds(first_rounds[j][r] if isinstance(j, int) and j in first_rounds else hid_ps)

        def expert_bank(j, t):
            return first_experts[t] if first(j) else moe_ps

        block = ctx.enter_context(nc.Block())

        @block.sync
        def _(sp):
            sp.dma_start(cond_col[:, :], cond.rearrange("(b o) -> b o", o=1)).then_inc(cond_col_landed, 16)
            sp.dma_start(cond_b[:, :], cond[0:TOK // C].rearrange("(o b) -> o b", o=1)
                         .to_broadcast([P, TOK // C])).then_inc(cond_landed, 16)
            sp.dma_start(x_sb[:, groups(0), :], x_rows[:, groups(0), :]).then_inc(x_landed[0], 16)
            sp.wait_ge(gathered_all, 16)
            sp.dma_start(w_by_batch, w_all).then_inc(w_written, 16)
            sp.dma_start(x_sb[:, groups(1), :], x_rows[:, groups(1), :]).then_inc(x_landed[1], 16)
            sp.dma_start(eg_raw[:, :, 0:T], expert_w.rearrange("(k p) h -> p k h", p=P)).then_inc(eg_landed, 16)
            sp.dma_start(eg_raw[:, :, T:EG], gate_w.rearrange("(k p) e -> p k e", p=P)).then_inc(eg_landed, 16)
            sp.wait_ge(w_written, 16)
            sp.dma_start(w_raw[:, TILES:GROUPS, :],
                         w_by_batch.rearrange("b (c d) -> (b c) d", c=C).rearrange("(g p) d -> p g d", p=P)
                         [:, TILES:GROUPS, :]).then_inc(w_landed, 16)
            sp.dma_start(beta_b[:, :], beta.rearrange("(o t) -> o t", o=1).to_broadcast([P, T])) \
                .then_inc(ln_landed, 16)
            sp.dma_start(gamma_b[:, :], gamma.rearrange("(o t) -> o t", o=1).to_broadcast([P, T])) \
                .then_inc(ln_landed, 16)
            sp.dma_start(down_raw[:, :, :], down_w.rearrange("(c p) h -> p c h", p=P)).then_inc(down_landed, 16)
            with sp.Fori(1, BLOCKS // 2) as i:
                for par in range(2):
                    sp.wait_ge(x_landed[par], 16 * i)
                    sp.dma_start(x_sb[:, groups(2 * i + par), :], x_rows[:, groups(2 * i + par), :]) \
                        .then_inc(x_landed[par], 16)

            def store(j, par):
                sp.wait_ge(result_done, TILES * j + TILES)
                sp.dma_start(out_rows[:, groups(j), :], result[:, par, :, :]).then_inc(result_moved[par], 16)

            with sp.Fori(0, BLOCKS // 2 - 1) as i:
                store(2 * i, 0)
                store(2 * i + 1, 1)
            store(BLOCKS - 2, 0)
            for t in range(TILES):
                j = BLOCKS - 1
                sp.wait_ge(result_done, TILES * j + t + 1)
                sp.dma_start(out_rows[:, group(j, t), :], result[:, 1, t:t + 1, :]).then_inc(result_moved[1], 16)
            sp.wait_ge(result_moved[0], 16 * (BLOCKS // 2 + 1))
            sp.wait_ge(result_moved[1], 16 * (BLOCKS // 2 + TILES))

        @block.tensor
        def _(pe):
            def conditioning(j, r):
                if r == 0:
                    pe.wait_ge(x_hi_done, j + 1)
                    pe.wait_ge(x_lo_done, j + 1)
                    pe.wait_ge(wd_done, 2 * j + 2)
                if not isinstance(j, int) or j > 1:
                    pe.wait_ge(hid_hi_done, ROUNDS * j + r)
                    pe.wait_ge(hid_lo_done, ROUNDS * j + r)
                elif j == 1 and r == 2:
                    pe.wait_ge(hid_hi_done, ROUNDS + 1)
                    pe.wait_ge(hid_lo_done, ROUNDS + 1)
                elif j == 1 and r == 3:
                    pe.wait_ge(moe_scaled, 2)
                k, pair = r // 2, r % 2
                for g in range(2):
                    t = 2 * pair + g
                    dst = round_bank(j, r)[:, g, :, :].rearrange("p s n -> p (s n)")
                    pe.matmul(dst, xs_hi[:, t, P * k:P * k + P],
                              wd_hl[:, t, :, :, :].rearrange("p s q d -> p (s q d)"), start=True, stop=False)
                    mm = pe.matmul(dst[:, P:2 * P], xs_lo[:, t, P * k:P * k + P],
                                   wd_hl[:, t, 0, :, :].rearrange("p q d -> p (q d)"), start=False, stop=True)
                mm.then_inc(hid_done, 1)

            def up(j, par, c):
                if c == 0:
                    pe.wait_ge(hid_hi_done, ROUNDS * j + ROUNDS)
                    pe.wait_ge(hid_lo_done, ROUNDS * j + ROUNDS)
                if first(j) and c == 0:
                    for k in range(K):
                        pe.wait_ge(up_hi_ready, k + 1)
                        pe.wait_ge(up_lo_ready[k], 1)
                wait(pe, square_done, CH * j + c - UPB + 1)
                dst = up_ps[c % UPB][:, :]
                for k in range(K):
                    w_h = up_hi[:, k, P * c:P * c + P]
                    w_l = up_lo[:, k, P * c:P * c + P]
                    pe.matmul(dst, w_l, hid_hi[:, par, k, :], start=(k == 0), stop=False)
                    pe.matmul(dst, w_h, hid_lo[:, par, k, :], start=False, stop=False)
                    mm = pe.matmul(dst, w_h, hid_hi[:, par, k, :], start=False, stop=(k == K - 1))
                mm.then_inc(up_done, 1)

            def down(j, par, t, half):
                if half == 0:
                    if t > 1 or isinstance(j, int):
                        wait(pe, y_done, TILES * j + t - 1)
                if t == 0 and (first(j) or not isinstance(j, int)):
                    pe.wait_ge(down_hi_ready, half + 1)
                    pe.wait_ge(down_lo_ready, half + 1)
                if t == 0:
                    pe.wait_ge(sq_hi_done, CH * j + HALF * (half + 1))
                    pe.wait_ge(sq_lo_done, CH * j + HALF * (half + 1))
                dst = down_ps[t % 2]
                for c in range(HALF * half, HALF * half + HALF):
                    pe.matmul(dst[:, :], sq_hi[:, par, c, P * t:P * t + P],
                              down_hl[:, c, :, :].rearrange("p s t -> p (s t)"),
                              start=(c == 0), stop=False)
                    mm = pe.matmul(dst[:, T:2 * T], sq_lo[:, par, c, P * t:P * t + P], down_hl[:, c, 0, :],
                                   start=False, stop=(c == CH - 1))
                if half == 1:
                    mm.then_inc(down_done, 1)

            def experts(j, par, t):
                if first(j) and t == 0:
                    pe.wait_ge(eg_hi_ready, 1)
                    pe.wait_ge(eg_lo_ready, 1)
                if first(j) and t == 2:
                    pe.wait_ge(hid_hi_done, ROUNDS + 2)
                    pe.wait_ge(hid_lo_done, ROUNDS + 2)
                elif first(j):
                    wait(pe, moe_scaled, t // 3)
                else:
                    pe.wait_ge(moe_scaled, TILES * j + t)
                dst = expert_bank(j, t)[:, 0:EG]
                for k in range(K):
                    a_hi = hid_hi[:, par, k, P * t:P * t + P]
                    a_lo = hid_lo[:, par, k, P * t:P * t + P]
                    pe.matmul(dst, a_lo, eg_hi[:, k, :], start=(k == 0), stop=False)
                    pe.matmul(dst, a_hi, eg_lo[:, k, :], start=False, stop=False)
                    mm = pe.matmul(dst, a_hi, eg_hi[:, k, :], start=False, stop=(k == K - 1))
                mm.then_inc(moe_done, 1)

            def step(j, par):
                for c in range(CH):
                    if has_up(j):
                        up(j, par, c)
                    if not first(j):
                        down(j - 1, 1 - par, c // 2, c % 2)
                    if has_next(j) and c in ROUND_AT:
                        conditioning(j + 1, ROUND_AT.index(c))
                    if has_up(j) and c % 2 == 1:
                        experts(j, par, c // 2)

            pe.wait_ge(x_landed[0], 16)
            for _ in range(WARM):
                pe.matmul(up_ps[0][:, :], x_sb[:, 0, 0:P], x_sb[:, 0:2, :].rearrange("p g t -> p (g t)"),
                          start=True, stop=True)
            for r in range(ROUNDS):
                conditioning(0, r)
            steps(pe, step)

        @block.scalar
        def _(act):
            act.wait_ge(cond_landed, 16)
            for k in range(K):
                act.dma_start(up_raw[:, k, :], up_w[P * k:P * k + P, :]).then_inc(result_moved[k], 16)

            def split_x(j, par):
                act.wait_ge(x_landed[par], 16 * (j // 2 + 1) if isinstance(j, int) else 8 * (j - par) + 16)
                wait(act, hid_done, ROUNDS * j)
                act.activation(xs_hi[:, :, :], x_sb[:, groups(j), :], ACT.Copy).then_inc(x_hi_done, 1)

            def hidden(j, par, r):
                k, pair = r // 2, r % 2
                act.wait_ge(hid_done, ROUNDS * j + r + 1)
                act.activation(hid_hi[:, par, k, 2 * P * pair:2 * P * (pair + 1)].rearrange("p (g n) -> p g n", g=2),
                               round_bank(j, r)[:, :, 0, :], ACT.Copy).then_inc(hid_hi_done, 1)

            def scale_moe(j, t):
                act.wait_ge(scale_done, TILES * j + t + 1)
                act.activation(moe[:, t, :], expert_bank(j, t)[:, 0:T], ACT.Copy, scale=scale[:, t % 2:t % 2 + 1]) \
                    .then_inc(moe_scaled, 1)

            def step(j, par):
                for c in range(CH):
                    if has_next(j) and c == 0:
                        split_x(j + 1, 1 - par)
                    if has_next(j) and c - 1 in ROUND_AT:
                        hidden(j + 1, 1 - par, ROUND_AT.index(c - 1))
                    if has_up(j):
                        n = CH * j + c
                        act.wait_ge(up_done, n + 1)
                        wait(act, square_done, n - 1)
                        act.activation(relu[:, c % 2, :], up_ps[c % UPB][:, :], ACT.Relu).then_inc(relu_done, 1)
                    if has_up(j):
                        act.wait_ge(relu_done, n + 1)
                        act.activation(sq_hi[:, par, c, :], relu[:, c % 2, :], ACT.Square) \
                            .then_inc(sq_hi_done, 1)
                    if has_up(j) and c % 2 == 0 and c > 0:
                        scale_moe(j, c // 2 - 1)
                    if not first(j) and c == 0:
                        scale_moe(j - 1, TILES - 1)
                    if first(j) and c in (5, 7):
                        split_down((c - 5) // 2)

            def split_down(h):
                if h == 0:
                    act.wait_ge(down_landed, 16)
                part = slice(HALF * h, HALF * h + HALF)
                act.activation(down_hl[:, part, 0, :], down_raw[:, part, :], ACT.Copy).then_inc(down_hi_ready, 1)

            def split_up(k):
                act.wait_ge(result_moved[k], 16)
                act.activation(up_hi[:, k, :], up_raw[:, k, :], ACT.Copy).then_inc(up_hi_ready, 1)

            split_x(0, 0)
            split_up(0)
            act.wait_ge(gathered_first, 16 * TILES)
            act.activation(w_hi[:, 0:TILES, :].bitcast(f32r), w_raw[:, 0:TILES, :], ACT.Copy) \
                .then_inc(w_hi_ready, 1)
            split_up(1)
            for r in range(ROUNDS):
                hidden(0, 0, r)
            act.wait_ge(eg_landed, 32)
            act.activation(eg_hi[:, :, :], eg_raw[:, :, :], ACT.Copy).then_inc(eg_hi_ready, 1)
            act.wait_ge(w_landed, 16)
            act.activation(w_hi[:, TILES:GROUPS, :].bitcast(f32r), w_raw[:, TILES:GROUPS, :], ACT.Copy) \
                .then_inc(w_hi_ready, 1)
            steps(act, step)

        @block.vector
        def _(dve):
            def gather_rows():
                dve.wait_ge(cond_landed, 16)
                dve.wait_ge(chan_ready, 1)
                of_batch = cond_b[:, :].rearrange("p (g q) -> p g q", q=Q)
                for q in range(Q):
                    part = slice(C * q, C * q + C)
                    dve.tensor_scalar(rows[part, :], of_batch[part, :, q], float(C), chan[part, q:q + 1],
                                      ALU.mult, ALU.add).then_inc(rows_ready, 1)

            def spread(j, s, src):
                wide = src[:, groups(j), :].unsqueeze(2).to_broadcast([P, TILES, Q, D])
                dve.tensor_tensor(wd_hl[:, :, s, :, :], wide, mask[:, :, :, :], ALU.mult).then_inc(wd_done, 1)

            def spread_w(j):
                dve.wait_ge(w_lo_rest_ready, 1)
                wait(dve, hid_done, ROUNDS * j)
                spread(j, 0, w_hi)
                spread(j, 1, w_raw)

            def hidden(j, par, r):
                k, pair = r // 2, r % 2
                cols = slice(2 * P * pair, 2 * P * (pair + 1))
                dve.wait_ge(hid_hi_done, ROUNDS * j + r + 1)
                dve.tensor_tensor(hid_rest[:, r % 2, :, :], round_bank(j, r)[:, :, 0, :],
                                  hid_hi[:, par, k, cols].bitcast(f32).rearrange("p (g n) -> p g n", g=2),
                                  ALU.subtract).then_inc(hid_rest_done, 1)
                dve.wait_ge(hid_rest_done, ROUNDS * j + r + 1)
                dve.tensor_tensor(hid_lo[:, par, k, cols].rearrange("p (g n) -> p g n", g=2), hid_rest[:, r % 2, :, :],
                                  round_bank(j, r)[:, :, 1, :], ALU.add).then_inc(hid_lo_done, 1)

            def gate(j, t):
                n = TILES * j + t
                if isinstance(j, int) and j == BLOCKS - 1 and t == TILES - 1:
                    dve.wait_ge(moe_done, n + 1)
                dve.max(top8[:, :], expert_bank(j, t)[:, T:EG]).then_inc(top8_done, 1)
                dve.wait_ge(top8_done, n + 1)
                wait(dve, moe_scaled, n - 1)
                dve.tensor_tensor(scale[:, t % 2:t % 2 + 1], top8[:, 0:1], top8[:, 1:2], ALU.add) \
                    .then_inc(scale_done, 1)

            def total(j, t):
                n = TILES * j + t
                dve.wait_ge(down_done, n + 1)
                dve.wait_ge(moe_scaled, n + 1)
                dve.tensor_tensor(y_half[:, :], down_ps[t % 2][:, T:2 * T], moe[:, t, :], ALU.add) \
                    .then_inc(y_half_done, 1)
                dve.wait_ge(y_half_done, n + 1)
                dve.tensor_tensor(y[:, t % 2, :], down_ps[t % 2][:, 0:T], y_half[:, :], ALU.add) \
                    .then_inc(y_done, 1)
                dve.wait_ge(y_done, n + 1)
                dve.bn_stats(stats[:, :], y[:, t % 2, :]).then_inc(bn_done, 1)
                wait_apart(dve, bn_done, n + 1, mask_ready, Q)
                dve.bn_aggr(meanvar[:, t % 2, :], stats[:, :]).then_inc(stats_done, 1)

            def centre(j, t):
                n = TILES * j + t
                dve.wait_ge(stats_done, n + 1)
                dve.scalar_tensor_tensor(y[:, t % 2, :], y[:, t % 2, :], meanvar[:, t % 2, 0:1], gamma_b[:, :],
                                         ALU.subtract, ALU.mult).then_inc(scaled_done, 1)

            def finish(j, par, t):
                n = TILES * j + t
                dve.wait_ge(scaled_done, n + 1)
                dve.wait_ge(rstd_done, n + 1)
                dve.wait_ge(xb_done, j + 1)
                if t == 0:
                    dve.wait_ge(result_moved[par], 16 * (j // 2) + 16 if isinstance(j, int) else 8 * (j - par) + 16)
                dve.scalar_tensor_tensor(result[:, par, t, :], y[:, t % 2, :], rstd[:, t % 2:t % 2 + 1],
                                         x_sb[:, group(j, t), :].rearrange("p o t -> p (o t)"),
                                         ALU.mult, ALU.add).then_inc(result_done, 1)

            def step(j, par):
                for c in range(CH):
                    if has_next(j) and c - 1 in ROUND_AT:
                        hidden(j + 1, 1 - par, ROUND_AT.index(c - 1))
                    if has_up(j):
                        n = CH * j + c
                        dve.wait_ge(relu_done, n + 1)
                        wait(dve, sq_lo_done, n - 1)
                        dve.scalar_tensor_tensor(square[:, c % 2, :], up_ps[c % UPB][:, :], 0.0,
                                                 relu[:, c % 2, :], ALU.max, ALU.mult).then_inc(square_done, 1)
                    if has_up(j) and c % 2 == 0 and c > 0:
                        gate(j, c // 2 - 1)
                    if not first(j) and c == 0:
                        gate(j - 1, TILES - 1)
                    if has_next(j) and c == 0:
                        spread_w(j + 1)
                    if first(j) and c in (5, 7):
                        split_down((c - 5) // 2)
                    if not first(j) and c % 2 == 1:
                        total(j - 1, c // 2)
                        centre(j - 1, c // 2)
                        if c > 1:
                            finish(j - 1, 1 - par, c // 2 - 1)
                if not first(j):
                    finish(j - 1, 1 - par, TILES - 1)

            def split_down(h):
                part = slice(HALF * h, HALF * h + HALF)
                dve.wait_ge(down_hi_ready, h + 1)
                dve.tensor_tensor(down_hl[:, part, 1, :], down_raw[:, part, :], down_hl[:, part, 0, :].bitcast(f32),
                                  ALU.subtract).then_inc(down_lo_ready, 1)

            gather_rows()
            dve.memset(mask[:, :, :, :], 0.0).then_inc(zeroed, 1)
            dve.wait_ge(zeroed, 1)
            for q in range(Q):
                dve.memset(mask[C * q:C * q + C, :, q, :], 1.0).then_inc(mask_ready, 1)
            dve.wait_ge(mask_ready, Q)
            dve.wait_ge(up_hi_ready, 1)
            dve.tensor_tensor(up_lo[:, 0, :], up_raw[:, 0, :], up_hi[:, 0, :].bitcast(f32), ALU.subtract) \
                .then_inc(up_lo_ready[0], 1)
            dve.wait_ge(gathered_first, 16 * TILES)
            spread(0, 0, w_raw)
            dve.wait_ge(w_hi_ready, 1)
            dve.tensor_tensor(w_hi[:, 0:TILES, :], w_raw[:, 0:TILES, :], w_hi[:, 0:TILES, :], ALU.subtract) \
                .then_inc(w_lo_ready, 1)
            dve.wait_ge(w_lo_ready, 1)
            spread(0, 1, w_hi)
            for r in range(ROUNDS):
                hidden(0, 0, r)
            dve.wait_ge(eg_hi_ready, 1)
            dve.tensor_tensor(eg_lo[:, :, :], eg_raw[:, :, :], eg_hi[:, :, :].bitcast(f32), ALU.subtract) \
                .then_inc(eg_lo_ready, 1)
            dve.wait_ge(ln_landed, 32)
            steps(dve, step)

        @block.gpsimd
        def _(pool):
            def split_x(j):
                wait_apart(pool, x_hi_done, j + 1, consts_ready, 2)
                pool.tensor_tensor(xs_lo[:, :, :], x_sb[:, groups(j), :], xs_hi[:, :, :].bitcast(f32),
                                   ALU.subtract).then_inc(x_lo_done, 1)

            def add_beta(j):
                wait_apart(pool, x_lo_done, j + 1, ln_landed, 32)
                pool.tensor_tensor(x_sb[:, groups(j), :], x_sb[:, groups(j), :],
                                   beta_b[:, :].unsqueeze(1).to_broadcast([P, TILES, T]),
                                   ALU.add).then_inc(xb_done, 1)

            def inverse_std(j, t):
                n = TILES * j + t
                pool.wait_ge(stats_done, n + 1)
                pool.tensor_tensor(var_eps[:, t % 2:t % 2 + 1], meanvar[:, t % 2, 1:2], eps[:, :], ALU.add) \
                    .then_inc(var_eps_done, 1)
                pool.wait_ge(var_eps_done, n + 1)
                pool.tensor_tensor(rstd[:, t % 2:t % 2 + 1], var_eps[:, t % 2:t % 2 + 1], minus_half[:, :], ALU.pow) \
                    .then_inc(rstd_done, 1)

            def step(j, par):
                for c in range(CH):
                    if has_next(j) and c == 0:
                        split_x(j + 1)
                    if has_up(j):
                        n = CH * j + c
                        pool.wait_ge(square_done, n + 1)
                        pool.wait_ge(sq_hi_done, n + 1)
                        pool.tensor_tensor(sq_lo[:, par, c, :], square[:, c % 2, :],
                                           sq_hi[:, par, c, :].bitcast(f32), ALU.subtract).then_inc(sq_lo_done, 1)
                    if not first(j) and c % 2 == 0 and c > 0:
                        inverse_std(j - 1, c // 2 - 1)
                if not first(j):
                    inverse_std(j - 1, TILES - 1)
                if has_up(j):
                    add_beta(j)

            pool.iota(chan[:, :], pattern=[[-C, Q]], base=0, channel_multiplier=1).then_inc(chan_ready, 1)
            pool.memset(minus_half[:, :], -0.5).then_inc(consts_ready, 1)
            pool.memset(eps[:, :], EPS).then_inc(consts_ready, 1)
            pool.wait_ge(cond_col_landed, 16)
            pool.indirect_dma_start(
                out=w_all, out_offset=None, in_=cond_w.rearrange("s c d -> s (c d)"),
                in_offset=bass.IndirectOffsetOnAxis(ap=cond_col[:, 0:1], axis=0)).then_inc(gathered_all, 16)
            pool.wait_ge(rows_ready, Q)
            for g in range(TILES):
                pool.indirect_dma_start(
                    out=w_raw[:, g, :], out_offset=None, in_=table,
                    in_offset=bass.IndirectOffsetOnAxis(ap=rows[:, g:g + 1], axis=0)).then_inc(gathered_first, 16)
            split_x(0)
            pool.wait_ge(up_hi_ready, 2)
            pool.tensor_tensor(up_lo[:, 1, :], up_raw[:, 1, :], up_hi[:, 1, :].bitcast(f32), ALU.subtract) \
                .then_inc(up_lo_ready[1], 1)
            pool.wait_ge(w_hi_ready, 2)
            pool.tensor_tensor(w_raw[:, TILES:GROUPS, :], w_raw[:, TILES:GROUPS, :], w_hi[:, TILES:GROUPS, :],
                               ALU.subtract).then_inc(w_lo_rest_ready, 1)
            pool.wait_ge(ln_landed, 32)
            pool.wait_ge(consts_ready, 2)
            steps(pool, step)


_INS = ["x", "itok_B_1_198", "L0_cond_weights", "L0_ffn_gate_w", "L0_ffn_up_w", "L0_ffn_down_w",
        "L0_ffn_expert_weight", "L0_ffn_ln_gamma", "L0_ffn_ln_beta"]
_OUT = ((ROWS_B, C, T), "float32")


def kernel(**inputs):
    import numpy as _np
    import concourse.bacc as _bacc
    from concourse import mybir as _mybir
    from concourse.bass_utils import run_bass_kernel_spmd as _run

    nc = _bacc.Bacc("TRN2", target_bir_lowering=False, num_devices=1)
    arrays, args = {}, []
    for name in _INS:
        a = _np.ascontiguousarray(inputs[name])
        arrays[f"in_{name}_dram"] = a
        args.append(nc.dram_tensor(f"in_{name}_dram", a.shape, _mybir.dt.from_np(a.dtype), kind="ExternalInput").ap())
    shape, dtype = _OUT
    args.append(nc.dram_tensor("out_0_dram", shape, _mybir.dt.from_np(_np.dtype(dtype)), kind="ExternalOutput").ap())
    adaln_ffn(nc, *args)
    r = _run(nc, [arrays], core_ids=[0])
    return r.results[0]["out_0_dram"]
```

```python
from contextlib import ExitStack

import concourse.bass as bass
from concourse import mybir

P = 128
ROWS_B, C, T, D = 128, 32, 256, 32
INTER, NEXP = 1024, 8
EPS = 1e-5
Q = P // C
GROUPS = ROWS_B // Q
TILES = 4
BLOCKS = GROUPS // TILES
TOK = TILES * P
K = T // P
CH = INTER // P
EG = T + NEXP
UPB = 4
HALF = CH // 2
WARM_GATHER, WARM_SPLIT = 6, 2


def adaln_ffn(nc, x, cond, cond_w, gate_w, up_w, down_w, expert_w, gamma, beta, out):
    f32, f32r, i32 = mybir.dt.float32, mybir.dt.float32r, mybir.dt.int32
    ALU, ACT = mybir.AluOpType, mybir.ActivationFunctionType

    x_rows = x.rearrange("b c t -> (b c) t").rearrange("(g p) t -> p g t", p=P)
    out_rows = out.rearrange("b c t -> (b c) t").rearrange("(g p) t -> p g t", p=P)
    table = cond_w.rearrange("s c d -> (s c) d")

    ctx = ExitStack()
    with ctx:
        def sb(name, shape, dt=f32):
            return ctx.enter_context(nc.sbuf_tensor(name, shape, dt))

        def bank(name):
            return ctx.enter_context(nc.psum_tensor(name, [P, 512], f32))

        def sem(name):
            return ctx.enter_context(nc.semaphore(name))

        up_hi = sb("up_hi", [P, K, INTER], f32r)
        up_lo = sb("up_lo", [P, K, INTER], f32r)
        down_hl = sb("down_hl", [P, CH, 2, T], f32r)
        eg_hi = sb("eg_hi", [P, K, EG], f32r)
        eg_lo = sb("eg_lo", [P, K, EG], f32r)
        down_raw = sb("down_raw", [P, CH, T])
        eg_raw = sb("eg_raw", [P, K, EG])
        gamma_b = sb("gamma_b", [P, T])
        beta_b = sb("beta_b", [P, T])
        x_sb = sb("x_sb", [P, GROUPS, T])
        cond_b = sb("cond_b", [P, TOK // C], i32)
        cond_col = sb("cond_col", [P, 1], i32)
        chan = sb("chan", [P, Q], i32)
        rows = sb("rows", [P, TILES], i32)
        w_raw = sb("w_raw", [P, GROUPS, D])
        w_hi = sb("w_hi", [P, GROUPS, D])
        mask = sb("mask", [P, TILES, Q, D])
        wd_hl = sb("wd_hl", [P, TILES, 2, Q, D], f32r)
        xs_hi = sb("xs_hi", [P, TILES, T], f32r)
        xs_lo = sb("xs_lo", [P, TILES, T], f32r)
        hid_hi = sb("hid_hi", [P, 2, K, TOK], f32r)
        hid_lo = sb("hid_lo", [P, 2, K, TOK], f32r)
        hid_rest = sb("hid_rest", [P, 2, 2, P])
        relu = sb("relu", [P, 2, TOK])
        square = sb("square", [P, 2, TOK])
        sq_hi = sb("sq_hi", [P, 2, CH, TOK], f32r)
        sq_lo = sb("sq_lo", [P, 2, CH, TOK], f32r)
        top8 = sb("top8", [P, 8])
        scale = sb("scale", [P, 2])
        moe = sb("moe", [P, TILES, T])
        y_half = sb("y_half", [P, T])
        y = sb("y", [P, 2, T])
        stats = sb("stats", [P, 6])
        meanvar = sb("meanvar", [P, 2, 2])
        var_eps = sb("var_eps", [P, 2])
        minus_half = sb("minus_half", [P, 1])
        eps = sb("eps", [P, 1])
        rstd = sb("rstd", [P, 2])
        result = sb("result", [P, 2, TILES, T])
        up_raw = result[:, :, :, :].rearrange("p a b t -> p (a b t)").rearrange("p (k i) -> p k i", k=K)

        w_all = moe[:, :, :].rearrange("p a t -> p (a t)")
        w_by_batch = nc.dram_tensor("w_by_batch", [ROWS_B, C * D], f32, kind="Internal").ap()

        up_ps = [bank(f"up_ps{n}") for n in range(UPB)]
        hid_ps = bank("hid_ps")
        moe_ps = bank("moe_ps")
        down_ps = [bank(f"down_ps{n}") for n in range(2)]

        x_landed = [sem("x_landed_even"), sem("x_landed_odd")]
        cond_landed, cond_col_landed, down_landed, eg_landed, ln_landed = map(
            sem, ("cond_landed", "cond_col_landed", "down_landed", "eg_landed", "ln_landed"))
        gathered_first = [sem("gathered_first_pair0"), sem("gathered_first_pair1")]
        gathered_all, w_written = sem("gathered_all"), sem("w_written")
        w_landed = [sem("w_landed_second"), sem("w_landed_rest")]
        result_moved = [sem("result_moved_even"), sem("result_moved_odd")]
        chan_ready, rows_ready, zeroed, mask_ready, consts_ready = map(
            sem, ("chan_ready", "rows_ready", "zeroed", "mask_ready", "consts_ready"))
        up_lo_ready = [sem("up_lo_ready_even"), sem("up_lo_ready_odd")]
        up_hi_ready, down_hi_ready, down_lo_ready, eg_hi_ready, eg_lo_ready = map(
            sem, ("up_hi_ready", "down_hi_ready", "down_lo_ready", "eg_hi_ready", "eg_lo_ready"))
        w_hi_ready, w_lo_ready, w_lo_rest_ready = map(
            sem, ("w_hi_ready", "w_lo_ready", "w_lo_rest_ready"))
        up_done, down_done, moe_done, hid_done = map(sem, ("up_done", "down_done", "moe_done", "hid_done"))
        relu_done, sq_hi_done, hid_hi_done, moe_scaled, x_hi_done = map(
            sem, ("relu_done", "sq_hi_done", "hid_hi_done", "moe_scaled", "x_hi_done"))
        square_done, hid_rest_done, hid_lo_done, top8_done, scale_done, wd_done = map(
            sem, ("square_done", "hid_rest_done", "hid_lo_done", "top8_done", "scale_done", "wd_done"))
        y_half_done, y_done, bn_done, stats_done, scaled_done, result_done = map(
            sem, ("y_half_done", "y_done", "bn_done", "stats_done", "scaled_done", "result_done"))
        sq_lo_done, x_lo_done, xb_done, var_eps_done, rstd_done = map(
            sem, ("sq_lo_done", "x_lo_done", "xb_done", "var_eps_done", "rstd_done"))

        def wait(eng, s, count):
            if not isinstance(count, int) or count > 0:
                eng.wait_ge(s, count)

        def wait_apart(eng, s, count, settled, settled_at):
            eng.wait_ge(settled, settled_at)
            eng.wait_ge(s, count)

        def steps(eng, step):
            step(0, 0)
            with eng.Fori(0, BLOCKS // 2 - 1) as i:
                step(2 * i + 1, 1)
                step(2 * i + 2, 0)
            step(BLOCKS - 1, 1)
            step(BLOCKS, 0)

        def first(j):
            return isinstance(j, int) and j == 0

        def last(j):
            return isinstance(j, int) and j == BLOCKS - 1

        def has_up(j):
            return not isinstance(j, int) or j < BLOCKS

        def has_next(j):
            return not isinstance(j, int) or j + 1 < BLOCKS

        def groups(j):
            return slice(TILES * j, TILES * j + TILES) if isinstance(j, int) else bass.ds(TILES * j, TILES)

        def group(j, t):
            return slice(TILES * j + t, TILES * j + t + 1) if isinstance(j, int) else bass.ds(TILES * j + t, 1)

        def rounds(bank_):
            return bank_[:, :].rearrange("p (g s n) -> p g s n", g=2, s=2)

        ROUNDS = 2 * K

        def round_at(j):
            return (3, 4, 5, 6) if first(j) else (2, 3, 5, 6)

        def pair_groups(pair):
            return slice(2 * pair, 2 * pair + 2)

        LATER_W = (slice(TILES, 2 * TILES), slice(2 * TILES, GROUPS))

        SPLIT_DOWN_AT = (3, 4, 7, 7)
        SPLIT_W_AT = (0, 1)
        W_REST_LO_AT = 4
        SPLIT_PARTS = len(SPLIT_DOWN_AT)

        def down_part(n):
            return slice(CH // SPLIT_PARTS * n, CH // SPLIT_PARTS * (n + 1))

        first_rounds = {0: [hid_ps, moe_ps, *down_ps], 1: [hid_ps, moe_ps, hid_ps, down_ps[0]]}
        first_experts = [moe_ps, *down_ps, moe_ps]

        def round_bank(j, r):
            return rounds(first_rounds[j][r] if isinstance(j, int) and j in first_rounds else hid_ps)

        def added_up(j):
            return first(j)

        def expert_bank(j, t):
            return first_experts[t] if first(j) else moe_ps

        block = ctx.enter_context(nc.Block())

        @block.sync
        def _(sp):
            sp.dma_start(cond_col[:, :], cond.rearrange("(b o) -> b o", o=1)).then_inc(cond_col_landed, 16)
            sp.dma_start(cond_b[:, :], cond[0:TOK // C].rearrange("(o b) -> o b", o=1)
                         .to_broadcast([P, TOK // C])).then_inc(cond_landed, 16)
            sp.dma_start(x_sb[:, groups(0), :], x_rows[:, groups(0), :]).then_inc(x_landed[0], 16)
            for k in range(K):
                sp.dma_start(up_raw[:, k, :], up_w[P * k:P * k + P, :]).then_inc(result_moved[k], 16)
            sp.wait_ge(result_moved[1], 16)
            sp.dma_start(x_sb[:, groups(1), :], x_rows[:, groups(1), :]).then_inc(x_landed[1], 16)
            sp.wait_ge(gathered_all, 16)
            sp.dma_start(w_by_batch, w_all).then_inc(w_written, 16)
            sp.dma_start(eg_raw[:, :, 0:T], expert_w.rearrange("(k p) h -> p k h", p=P)).then_inc(eg_landed, 16)
            sp.dma_start(eg_raw[:, :, T:EG], gate_w.rearrange("(k p) e -> p k e", p=P)).then_inc(eg_landed, 16)
            sp.wait_ge(w_written, 16)
            w_rows = w_by_batch.rearrange("b (c d) -> (b c) d", c=C).rearrange("(g p) d -> p g d", p=P)
            for n, part in enumerate(LATER_W):
                sp.dma_start(w_raw[:, part, :], w_rows[:, part, :]).then_inc(w_landed[n], 16)
            sp.dma_start(beta_b[:, :], beta.rearrange("(o t) -> o t", o=1).to_broadcast([P, T])) \
                .then_inc(ln_landed, 16)
            sp.dma_start(gamma_b[:, :], gamma.rearrange("(o t) -> o t", o=1).to_broadcast([P, T])) \
                .then_inc(ln_landed, 16)
            sp.dma_start(down_raw[:, :, :], down_w.rearrange("(c p) h -> p c h", p=P)).then_inc(down_landed, 16)
            with sp.Fori(1, BLOCKS // 2) as i:
                for par in range(2):
                    sp.wait_ge(x_landed[par], 16 * i)
                    sp.dma_start(x_sb[:, groups(2 * i + par), :], x_rows[:, groups(2 * i + par), :]) \
                        .then_inc(x_landed[par], 16)

            def store(j, par):
                sp.wait_ge(result_done, TILES * j + TILES)
                sp.dma_start(out_rows[:, groups(j), :], result[:, par, :, :]).then_inc(result_moved[par], 16)

            with sp.Fori(0, BLOCKS // 2 - 1) as i:
                store(2 * i, 0)
                store(2 * i + 1, 1)
            store(BLOCKS - 2, 0)
            for t in range(TILES):
                j = BLOCKS - 1
                sp.wait_ge(result_done, TILES * j + t + 1)
                sp.dma_start(out_rows[:, group(j, t), :], result[:, 1, t:t + 1, :]).then_inc(result_moved[1], 16)
            sp.wait_ge(result_moved[0], 16 * (BLOCKS // 2 + 1))
            sp.wait_ge(result_moved[1], 16 * (BLOCKS // 2 + TILES))

        @block.tensor
        def _(pe):
            def conditioning(j, r):
                if r == 0:
                    pe.wait_ge(x_hi_done, j + 1)
                    pe.wait_ge(x_lo_done, j + 1)
                    pe.wait_ge(wd_done, 2 if first(j) else 2 * j + 4)
                if first(j) and r == 2:
                    pe.wait_ge(wd_done, 4)
                if not isinstance(j, int) or j > 1:
                    pe.wait_ge(hid_hi_done, ROUNDS * j + r)
                    pe.wait_ge(hid_lo_done, ROUNDS * j + r)
                elif j == 1 and r == 2:
                    pe.wait_ge(hid_hi_done, ROUNDS + 1)
                    pe.wait_ge(hid_lo_done, ROUNDS + 1)
                elif j == 1 and r in (1, 3):
                    pe.wait_ge(moe_scaled, (r + 1) // 2)
                pair, k = r // 2, r % 2
                for g in range(2):
                    t = 2 * pair + g
                    dst = round_bank(j, r)[:, g, :, :].rearrange("p s n -> p (s n)")
                    if added_up(j):
                        for s, x_part in enumerate((xs_hi, xs_hi, xs_lo)):
                            mm = pe.matmul(dst[:, 0:P], x_part[:, t, P * k:P * k + P],
                                           wd_hl[:, t, s % 2, :, :].rearrange("p q d -> p (q d)"),
                                           start=(s == 0), stop=(s == 2))
                        continue
                    pe.matmul(dst, xs_hi[:, t, P * k:P * k + P],
                              wd_hl[:, t, :, :, :].rearrange("p s q d -> p (s q d)"), start=True, stop=False)
                    mm = pe.matmul(dst[:, P:2 * P], xs_lo[:, t, P * k:P * k + P],
                                   wd_hl[:, t, 0, :, :].rearrange("p q d -> p (q d)"), start=False, stop=True)
                mm.then_inc(hid_done, 1)

            def up(j, par, c):
                if c == 0:
                    pe.wait_ge(hid_hi_done, ROUNDS * j + ROUNDS)
                    pe.wait_ge(hid_lo_done, ROUNDS * j + ROUNDS)
                if first(j) and c == 0:
                    for k in range(K):
                        pe.wait_ge(up_hi_ready, k + 1)
                        pe.wait_ge(up_lo_ready[k], 1)
                wait(pe, square_done, CH * j + c - UPB + 1)
                dst = up_ps[c % UPB][:, :]
                for k in range(K):
                    w_h = up_hi[:, k, P * c:P * c + P]
                    w_l = up_lo[:, k, P * c:P * c + P]
                    pe.matmul(dst, w_l, hid_hi[:, par, k, :], start=(k == 0), stop=False)
                    pe.matmul(dst, w_h, hid_lo[:, par, k, :], start=False, stop=False)
                    mm = pe.matmul(dst, w_h, hid_hi[:, par, k, :], start=False, stop=(k == K - 1))
                mm.then_inc(up_done, 1)

            def down(j, par, t, half):
                if half == 0:
                    if t > 1 or isinstance(j, int):
                        wait(pe, y_done, TILES * j + t - 1)
                if t == 0 and (first(j) or not isinstance(j, int)):
                    pe.wait_ge(down_hi_ready, SPLIT_PARTS // 2 * (half + 1))
                    pe.wait_ge(down_lo_ready, SPLIT_PARTS // 2 * (half + 1))
                if t == 0:
                    pe.wait_ge(sq_hi_done, CH * j + HALF * (half + 1))
                    pe.wait_ge(sq_lo_done, CH * j + HALF * (half + 1))
                dst = down_ps[t % 2]
                for c in range(HALF * half, HALF * half + HALF):
                    if last(j):
                        pe.matmul(dst[:, 0:T], sq_hi[:, par, c, P * t:P * t + P], down_hl[:, c, 0, :],
                                  start=(c == 0), stop=False)
                        pe.matmul(dst[:, 0:T], sq_hi[:, par, c, P * t:P * t + P], down_hl[:, c, 1, :],
                                  start=False, stop=False)
                        mm = pe.matmul(dst[:, 0:T], sq_lo[:, par, c, P * t:P * t + P], down_hl[:, c, 0, :],
                                       start=False, stop=(c == CH - 1))
                        continue
                    pe.matmul(dst[:, :], sq_hi[:, par, c, P * t:P * t + P],
                              down_hl[:, c, :, :].rearrange("p s t -> p (s t)"),
                              start=(c == 0), stop=False)
                    mm = pe.matmul(dst[:, T:2 * T], sq_lo[:, par, c, P * t:P * t + P], down_hl[:, c, 0, :],
                                   start=False, stop=(c == CH - 1))
                if half == 1:
                    mm.then_inc(down_done, 1)

            def experts(j, par, t):
                if first(j) and t == 0:
                    pe.wait_ge(eg_hi_ready, 1)
                    pe.wait_ge(eg_lo_ready, 1)
                if first(j) and t == 3:
                    pe.wait_ge(hid_hi_done, ROUNDS + 2)
                    pe.wait_ge(hid_lo_done, ROUNDS + 2)
                elif not first(j):
                    pe.wait_ge(moe_scaled, TILES * j + t)
                dst = expert_bank(j, t)[:, 0:EG]
                for k in range(K):
                    a_hi = hid_hi[:, par, k, P * t:P * t + P]
                    a_lo = hid_lo[:, par, k, P * t:P * t + P]
                    pe.matmul(dst, a_lo, eg_hi[:, k, :], start=(k == 0), stop=False)
                    pe.matmul(dst, a_hi, eg_lo[:, k, :], start=False, stop=False)
                    mm = pe.matmul(dst, a_hi, eg_hi[:, k, :], start=False, stop=(k == K - 1))
                mm.then_inc(moe_done, 1)

            def step(j, par):
                for c in range(CH):
                    if has_up(j):
                        up(j, par, c)
                    if not first(j):
                        down(j - 1, 1 - par, c // 2, c % 2)
                    for r in range(ROUNDS):
                        if has_next(j) and c == round_at(j)[r]:
                            conditioning(j + 1, r)
                    if has_up(j) and c % 2 == 1:
                        experts(j, par, c // 2)

            def keep_warm(n):
                for _ in range(n):
                    pe.matmul(up_ps[0][:, 0:T], x_sb[:, 0, 0:P], x_sb[:, 0, :], start=True, stop=True)

            pe.wait_ge(x_landed[0], 16)
            keep_warm(WARM_GATHER)
            for r in range(ROUNDS):
                conditioning(0, r)
            keep_warm(WARM_SPLIT)
            steps(pe, step)

        @block.scalar
        def _(act):
            def split_x(j, par):
                act.wait_ge(x_landed[par], 16 * (j // 2 + 1) if isinstance(j, int) else 8 * (j - par) + 16)
                wait(act, hid_done, ROUNDS * j)
                act.activation(xs_hi[:, :, :], x_sb[:, groups(j), :], ACT.Copy).then_inc(x_hi_done, 1)

            def hidden(j, par, r):
                pair, k = r // 2, r % 2
                act.wait_ge(hid_done, ROUNDS * j + r + 1)
                act.activation(hid_hi[:, par, k, 2 * P * pair:2 * P * (pair + 1)].rearrange("p (g n) -> p g n", g=2),
                               round_bank(j, r)[:, :, 0, :], ACT.Copy).then_inc(hid_hi_done, 1)

            def scale_moe(j, t):
                act.wait_ge(scale_done, TILES * j + t + 1)
                act.activation(moe[:, t, :], expert_bank(j, t)[:, 0:T], ACT.Copy, scale=scale[:, t % 2:t % 2 + 1]) \
                    .then_inc(moe_scaled, 1)

            def step(j, par):
                for c in range(CH):
                    if has_next(j) and c == 0 and not first(j):
                        split_x(j + 1, 1 - par)
                    for r in range(ROUNDS):
                        if has_next(j) and c - 1 == round_at(j)[r]:
                            hidden(j + 1, 1 - par, r)
                    if has_up(j):
                        n = CH * j + c
                        act.wait_ge(up_done, n + 1)
                        wait(act, square_done, n - 1)
                        act.activation(relu[:, c % 2, :], up_ps[c % UPB][:, :], ACT.Relu).then_inc(relu_done, 1)
                    if has_up(j):
                        act.wait_ge(relu_done, n + 1)
                        act.activation(sq_hi[:, par, c, :], relu[:, c % 2, :], ACT.Square) \
                            .then_inc(sq_hi_done, 1)
                    for later in range(2):
                        if first(j) and c == SPLIT_W_AT[later]:
                            split_w(later)
                    if has_up(j) and c % 2 == (1 if first(j) else 0) and c > 1:
                        scale_moe(j, c // 2 - 1)
                    if not first(j) and c == 0:
                        scale_moe(j - 1, TILES - 1)
                    for part_no in range(SPLIT_PARTS):
                        if first(j) and c == SPLIT_DOWN_AT[part_no]:
                            split_down(part_no)

            def split_w(n):
                act.wait_ge(w_landed[n], 16)
                act.activation(w_hi[:, LATER_W[n], :].bitcast(f32r), w_raw[:, LATER_W[n], :], ACT.Copy) \
                    .then_inc(w_hi_ready, 1)

            def split_down(part_no):
                if part_no == 0:
                    act.wait_ge(down_landed, 16)
                part = down_part(part_no)
                act.activation(down_hl[:, part, 0, :], down_raw[:, part, :], ACT.Copy).then_inc(down_hi_ready, 1)

            def split_up(k):
                act.wait_ge(result_moved[k], 16)
                act.activation(up_hi[:, k, :], up_raw[:, k, :], ACT.Copy).then_inc(up_hi_ready, 1)

            split_x(0, 0)
            split_up(0)
            split_up(1)
            for pair in range(2):
                act.wait_ge(gathered_first[pair], 32)
                act.activation(w_hi[:, pair_groups(pair), :].bitcast(f32r), w_raw[:, pair_groups(pair), :], ACT.Copy) \
                    .then_inc(w_hi_ready, 1)
            for r in range(ROUNDS):
                hidden(0, 0, r)
            act.wait_ge(eg_landed, 32)
            act.activation(eg_hi[:, :, :], eg_raw[:, :, :], ACT.Copy).then_inc(eg_hi_ready, 1)
            split_x(1, 1)
            steps(act, step)

        @block.vector
        def _(dve):
            def gather_rows():
                dve.wait_ge(cond_landed, 16)
                dve.wait_ge(chan_ready, 1)
                of_batch = cond_b[:, :].rearrange("p (g q) -> p g q", q=Q)
                for q in range(Q):
                    part = slice(C * q, C * q + C)
                    dve.tensor_scalar(rows[part, :], of_batch[part, :, q], float(C), chan[part, q:q + 1],
                                      ALU.mult, ALU.add).then_inc(rows_ready, 1)

            def spread_groups(part, s, src):
                wide = src.unsqueeze(2).to_broadcast([P, part.stop - part.start, Q, D])
                dve.tensor_tensor(wd_hl[:, part, s, :, :], wide, mask[:, part, :, :], ALU.mult).then_inc(wd_done, 1)

            def spread(j, s, src):
                spread_groups(slice(0, TILES), s, src[:, groups(j), :])

            def spread_w(j):
                if isinstance(j, int) and j == 1:
                    dve.wait_ge(w_hi_ready, 3)
                    dve.tensor_tensor(w_raw[:, LATER_W[0], :], w_raw[:, LATER_W[0], :], w_hi[:, LATER_W[0], :],
                                      ALU.subtract).then_inc(w_lo_ready, 1)
                    dve.wait_ge(w_lo_ready, 3)
                else:
                    dve.wait_ge(w_lo_rest_ready, 1)
                wait(dve, hid_done, ROUNDS * j)
                spread(j, 0, w_hi)
                spread(j, 1, w_raw)

            def hidden(j, par, r):
                pair, k = r // 2, r % 2
                cols = slice(2 * P * pair, 2 * P * (pair + 1))
                dve.wait_ge(hid_hi_done, ROUNDS * j + r + 1)
                if added_up(j):
                    dve.tensor_tensor(hid_lo[:, par, k, cols].rearrange("p (g n) -> p g n", g=2),
                                      round_bank(j, r)[:, :, 0, :],
                                      hid_hi[:, par, k, cols].bitcast(f32).rearrange("p (g n) -> p g n", g=2),
                                      ALU.subtract).then_inc(hid_lo_done, 1)
                    return
                dve.tensor_tensor(hid_rest[:, r % 2, :, :], round_bank(j, r)[:, :, 0, :],
                                  hid_hi[:, par, k, cols].bitcast(f32).rearrange("p (g n) -> p g n", g=2),
                                  ALU.subtract).then_inc(hid_rest_done, 1)
                dve.wait_ge(hid_rest_done, ROUNDS * (j - 1) + r + 1)
                dve.tensor_tensor(hid_lo[:, par, k, cols].rearrange("p (g n) -> p g n", g=2), hid_rest[:, r % 2, :, :],
                                  round_bank(j, r)[:, :, 1, :], ALU.add).then_inc(hid_lo_done, 1)

            def gate(j, t):
                n = TILES * j + t
                if last(j) and t == TILES - 1:
                    dve.wait_ge(moe_done, n + 1)
                dve.max(top8[:, :], expert_bank(j, t)[:, T:EG]).then_inc(top8_done, 1)
                dve.wait_ge(top8_done, n + 1)
                wait(dve, moe_scaled, n - 1)
                dve.tensor_tensor(scale[:, t % 2:t % 2 + 1], top8[:, 0:1], top8[:, 1:2], ALU.add) \
                    .then_inc(scale_done, 1)

            def total(j, t):
                n = TILES * j + t
                dve.wait_ge(down_done, n + 1)
                dve.wait_ge(moe_scaled, n + 1)
                if last(j):
                    dve.wait_ge(result_done, n - 1)
                    dve.tensor_tensor(y[:, t % 2, :], down_ps[t % 2][:, 0:T], moe[:, t, :], ALU.add) \
                        .then_inc(y_done, 1)
                else:
                    dve.tensor_tensor(y_half[:, :], down_ps[t % 2][:, T:2 * T], moe[:, t, :], ALU.add) \
                        .then_inc(y_half_done, 1)
                    dve.wait_ge(y_half_done, n + 1)
                    dve.tensor_tensor(y[:, t % 2, :], down_ps[t % 2][:, 0:T], y_half[:, :], ALU.add) \
                        .then_inc(y_done, 1)
                dve.wait_ge(y_done, n + 1)
                dve.bn_stats(stats[:, :], y[:, t % 2, :]).then_inc(bn_done, 1)
                wait_apart(dve, bn_done, n + 1, mask_ready, Q)
                dve.bn_aggr(meanvar[:, t % 2, :], stats[:, :]).then_inc(stats_done, 1)

            def centre(j, t):
                n = TILES * j + t
                dve.wait_ge(stats_done, n + 1)
                dve.scalar_tensor_tensor(y[:, t % 2, :], y[:, t % 2, :], meanvar[:, t % 2, 0:1], gamma_b[:, :],
                                         ALU.subtract, ALU.mult).then_inc(scaled_done, 1)

            def finish(j, par, t):
                n = TILES * j + t
                dve.wait_ge(scaled_done, n + 1)
                dve.wait_ge(rstd_done, n + 1)
                dve.wait_ge(xb_done, j + 1)
                if t == 0:
                    dve.wait_ge(result_moved[par], 16 * (j // 2) + 16 if isinstance(j, int) else 8 * (j - par) + 16)
                dve.scalar_tensor_tensor(result[:, par, t, :], y[:, t % 2, :], rstd[:, t % 2:t % 2 + 1],
                                         x_sb[:, group(j, t), :].rearrange("p o t -> p (o t)"),
                                         ALU.mult, ALU.add).then_inc(result_done, 1)

            def step(j, par):
                for c in range(CH):
                    for r in range(ROUNDS):
                        if has_next(j) and c - 1 == round_at(j)[r]:
                            hidden(j + 1, 1 - par, r)
                    if has_up(j):
                        n = CH * j + c
                        dve.wait_ge(relu_done, n + 1)
                        wait(dve, sq_lo_done, n - 1)
                        dve.scalar_tensor_tensor(square[:, c % 2, :], up_ps[c % UPB][:, :], 0.0,
                                                 relu[:, c % 2, :], ALU.max, ALU.mult).then_inc(square_done, 1)
                    if has_up(j) and c % 2 == 0 and c > 0:
                        gate(j, c // 2 - 1)
                    if not first(j) and c == 0:
                        gate(j - 1, TILES - 1)
                    if has_next(j) and c == (SPLIT_W_AT[0] if first(j) else 0):
                        spread_w(j + 1)
                    for part_no in range(SPLIT_PARTS):
                        if first(j) and c == SPLIT_DOWN_AT[part_no]:
                            split_down(part_no)
                    if not first(j) and c % 2 == 1:
                        total(j - 1, c // 2)
                        centre(j - 1, c // 2)
                        if c > 1:
                            finish(j - 1, 1 - par, c // 2 - 1)
                if first(j):
                    dve.wait_ge(ln_landed, 32)
                else:
                    finish(j - 1, 1 - par, TILES - 1)

            def split_down(part_no):
                part = down_part(part_no)
                dve.wait_ge(down_hi_ready, part_no + 1)
                dve.tensor_tensor(down_hl[:, part, 1, :], down_raw[:, part, :], down_hl[:, part, 0, :].bitcast(f32),
                                  ALU.subtract).then_inc(down_lo_ready, 1)

            gather_rows()
            dve.memset(mask[:, :, :, :], 0.0).then_inc(zeroed, 1)
            dve.wait_ge(zeroed, 1)
            for q in range(Q):
                dve.memset(mask[C * q:C * q + C, :, q, :], 1.0).then_inc(mask_ready, 1)
            dve.wait_ge(mask_ready, Q)
            dve.wait_ge(x_hi_done, 1)
            dve.tensor_tensor(xs_lo[:, :, :], x_sb[:, groups(0), :], xs_hi[:, :, :].bitcast(f32), ALU.subtract) \
                .then_inc(x_lo_done, 1)
            dve.wait_ge(up_hi_ready, 1)
            dve.tensor_tensor(up_lo[:, 0, :], up_raw[:, 0, :], up_hi[:, 0, :].bitcast(f32), ALU.subtract) \
                .then_inc(up_lo_ready[0], 1)
            for pair in range(2):
                part = pair_groups(pair)
                dve.wait_ge(gathered_first[pair], 32)
                spread_groups(part, 0, w_raw[:, part, :])
                dve.wait_ge(w_hi_ready, pair + 1)
                dve.tensor_tensor(w_hi[:, part, :], w_raw[:, part, :], w_hi[:, part, :], ALU.subtract) \
                    .then_inc(w_lo_ready, 1)
                dve.wait_ge(w_lo_ready, pair + 1)
                spread_groups(part, 1, w_hi[:, part, :])
            for r in range(ROUNDS):
                hidden(0, 0, r)
            dve.wait_ge(eg_hi_ready, 1)
            dve.tensor_tensor(eg_lo[:, :, :], eg_raw[:, :, :], eg_hi[:, :, :].bitcast(f32), ALU.subtract) \
                .then_inc(eg_lo_ready, 1)
            steps(dve, step)

        @block.gpsimd
        def _(pool):
            def split_x(j):
                wait_apart(pool, x_hi_done, j + 1, consts_ready, 2)
                pool.tensor_tensor(xs_lo[:, :, :], x_sb[:, groups(j), :], xs_hi[:, :, :].bitcast(f32),
                                   ALU.subtract).then_inc(x_lo_done, 1)

            def add_beta(j):
                wait_apart(pool, x_lo_done, j + 1, ln_landed, 32)
                pool.tensor_tensor(x_sb[:, groups(j), :], x_sb[:, groups(j), :],
                                   beta_b[:, :].unsqueeze(1).to_broadcast([P, TILES, T]),
                                   ALU.add).then_inc(xb_done, 1)

            def inverse_std(j, t):
                n = TILES * j + t
                pool.wait_ge(stats_done, n + 1)
                pool.tensor_tensor(var_eps[:, t % 2:t % 2 + 1], meanvar[:, t % 2, 1:2], eps[:, :], ALU.add) \
                    .then_inc(var_eps_done, 1)
                pool.wait_ge(var_eps_done, n + 1)
                pool.tensor_tensor(rstd[:, t % 2:t % 2 + 1], var_eps[:, t % 2:t % 2 + 1], minus_half[:, :], ALU.pow) \
                    .then_inc(rstd_done, 1)

            def step(j, par):
                for c in range(CH):
                    if has_next(j) and c == 0 and not first(j):
                        split_x(j + 1)
                    if has_up(j):
                        n = CH * j + c
                        pool.wait_ge(square_done, n + 1)
                        pool.wait_ge(sq_hi_done, n + 1)
                        pool.tensor_tensor(sq_lo[:, par, c, :], square[:, c % 2, :],
                                           sq_hi[:, par, c, :].bitcast(f32), ALU.subtract).then_inc(sq_lo_done, 1)
                    if first(j) and c == W_REST_LO_AT:
                        pool.wait_ge(w_hi_ready, 4)
                        pool.tensor_tensor(w_raw[:, LATER_W[1], :], w_raw[:, LATER_W[1], :], w_hi[:, LATER_W[1], :],
                                           ALU.subtract).then_inc(w_lo_rest_ready, 1)
                    if not first(j) and c % 2 == 0 and c > 0:
                        inverse_std(j - 1, c // 2 - 1)
                if not first(j):
                    inverse_std(j - 1, TILES - 1)
                if has_up(j):
                    add_beta(j)

            pool.iota(chan[:, :], pattern=[[-C, Q]], base=0, channel_multiplier=1).then_inc(chan_ready, 1)
            pool.memset(minus_half[:, :], -0.5).then_inc(consts_ready, 1)
            pool.memset(eps[:, :], EPS).then_inc(consts_ready, 1)
            pool.wait_ge(cond_col_landed, 16)
            pool.indirect_dma_start(
                out=w_all, out_offset=None, in_=cond_w.rearrange("s c d -> s (c d)"),
                in_offset=bass.IndirectOffsetOnAxis(ap=cond_col[:, 0:1], axis=0)).then_inc(gathered_all, 16)
            pool.wait_ge(rows_ready, Q)
            for g in range(TILES):
                pool.indirect_dma_start(
                    out=w_raw[:, g, :], out_offset=None, in_=table,
                    in_offset=bass.IndirectOffsetOnAxis(ap=rows[:, g:g + 1], axis=0)) \
                    .then_inc(gathered_first[g // 2], 16)
            pool.wait_ge(up_hi_ready, 2)
            pool.tensor_tensor(up_lo[:, 1, :], up_raw[:, 1, :], up_hi[:, 1, :].bitcast(f32), ALU.subtract) \
                .then_inc(up_lo_ready[1], 1)
            split_x(1)
            pool.wait_ge(consts_ready, 2)
            steps(pool, step)


_INS = ["x", "itok_B_1_198", "L0_cond_weights", "L0_ffn_gate_w", "L0_ffn_up_w", "L0_ffn_down_w",
        "L0_ffn_expert_weight", "L0_ffn_ln_gamma", "L0_ffn_ln_beta"]
_OUT = ((ROWS_B, C, T), "float32")


def kernel(**inputs):
    import numpy as _np
    import concourse.bacc as _bacc
    from concourse import mybir as _mybir
    from concourse.bass_utils import run_bass_kernel_spmd as _run

    nc = _bacc.Bacc("TRN2", target_bir_lowering=False, num_devices=1)
    arrays, args = {}, []
    for name in _INS:
        a = _np.ascontiguousarray(inputs[name])
        arrays[f"in_{name}_dram"] = a
        args.append(nc.dram_tensor(f"in_{name}_dram", a.shape, _mybir.dt.from_np(a.dtype), kind="ExternalInput").ap())
    shape, dtype = _OUT
    args.append(nc.dram_tensor("out_0_dram", shape, _mybir.dt.from_np(_np.dtype(dtype)), kind="ExternalOutput").ap())
    adaln_ffn(nc, *args)
    r = _run(nc, [arrays], core_ids=[0])
    return r.results[0]["out_0_dram"]
```
